# Optimizing a Trainium2 kernel written in Bass

```python
import numpy as np
import jax
import jax.numpy as jnp

def _softmax(x, axis=-1):
    return jax.nn.softmax(x, axis=axis)

def _gelu(x):
    return jax.nn.gelu(x, approximate=True)

def _silu(x):
    return jax.nn.silu(x)

def _sigmoid(x):
    return jax.nn.sigmoid(x)

def _layernorm(x, axis=-1, eps=1e-05):
    m = jnp.mean(x, axis=axis, keepdims=True)
    v = jnp.var(x, axis=axis, keepdims=True)
    return (x - m) / jnp.sqrt(v + eps)

def _scatter_add(tgt, idx, src, axis=0):
    return tgt.at[idx].add(src)

def _segment_sum(src, seg, n):
    return jax.ops.segment_sum(src, seg, n)
kernel_name = 'mk_adj_resnorm_d2_adj_r2_454210'

def setup_inputs(seed: int=0):
    np.random.seed(seed)
    _w = jnp.asarray

    def _rec_inputs():
        import jax
        import jax.numpy as jnp
        _gk = jax.random.key(seed)
        x = -0.0002928 + 1 * jax.random.normal(jax.random.fold_in(_gk, 1), (16, 512, 128), jnp.float32)
        _a = jax.random.bernoulli(jax.random.fold_in(_gk, 2), 0.03125, (16, 512, 512))
        _a = jnp.logical_or(_a, jnp.swapaxes(_a, -1, -2))
        _a = jnp.logical_or(_a, jnp.eye(512, dtype=bool))
        _af = _a.astype(jnp.float32)
        _af = _af * jax.random.uniform(jax.random.fold_in(_gk, 3), (16, 512, 512), jnp.float32, 0.05, 4.42607)
        adj = _af
        return (x, adj)
    x, adj = _rec_inputs()

    def _L0_gnn_setup():
        import math
        import jax, jax.numpy as jnp
        import numpy as np
        B, N, D, H = (32, 256, 128, 8)
        HD = D // H
        key = jax.random.key(seed)
        ks = jax.random.split(key, 9)
        h = jax.random.normal(ks[0], (B, N, D), dtype=jnp.float32)
        edge = jax.random.normal(ks[1], (B, N, N), dtype=jnp.float32)
        adj = jax.random.uniform(ks[2], (B, N, N)) < 0.5
        adj_mask = adj | jnp.eye(N, dtype=bool)[None]
        s = 1.0 / math.sqrt(D)
        W_q = jax.random.normal(ks[3], (D, D), dtype=jnp.float32) * s
        W_k = jax.random.normal(ks[4], (D, D), dtype=jnp.float32) * s
        W_v = jax.random.normal(ks[5], (D, D), dtype=jnp.float32) * s
        W_e = jax.random.normal(ks[6], (H, 1), dtype=jnp.float32)
        W_o = jax.random.normal(ks[7], (D, D), dtype=jnp.float32) * s
        return {'h': h, 'edge': edge, 'adj_mask': adj_mask, 'W_q': W_q, 'W_k': W_k, 'W_v': W_v, 'W_e': W_e, 'W_o': W_o}
    _L0_gnn_all = _L0_gnn_setup()
    _L0_gnn_in = {k: v for k, v in _L0_gnn_all.items() if k in ('W_q', 'W_k', 'W_v', 'W_e', 'W_o')}
    del _L0_gnn_all

    def _L1_gnn_setup():
        import jax, jax.numpy as jnp
        import numpy as np
        DIM = 128
        HEADS = 8
        BS = 8
        N = 512
        NEG = -1000000000.0
        key = jax.random.key(seed)
        ks = jax.random.split(key, 8)
        feats = jax.random.normal(ks[0], (BS, N, DIM), dtype=jnp.float32)
        adj_mat = (jax.random.uniform(ks[1], (BS, N, N)) < 0.1).astype(jnp.float32)
        s = 1.0 / np.sqrt(DIM)
        fc_w = jax.random.normal(ks[2], (DIM, DIM * HEADS), dtype=jnp.float32) * s
        fc_b = jnp.zeros((DIM * HEADS,), dtype=jnp.float32)
        q_w = jax.random.normal(ks[3], (DIM, 1), dtype=jnp.float32) * s
        q_b = jnp.zeros((1,), dtype=jnp.float32)
        k_w = jax.random.normal(ks[4], (DIM, 1), dtype=jnp.float32) * s
        k_b = jnp.zeros((1,), dtype=jnp.float32)
        fp_w = jax.random.normal(ks[5], (DIM * HEADS, DIM), dtype=jnp.float32) * (1.0 / np.sqrt(DIM * HEADS))
        fp_b = jnp.zeros((DIM,), dtype=jnp.float32)
        return {'feats': feats, 'adj_mat': adj_mat, 'fc_w': fc_w, 'fc_b': fc_b, 'q_w': q_w, 'q_b': q_b, 'k_w': k_w, 'k_b': k_b, 'fp_w': fp_w, 'fp_b': fp_b}
    _L1_gnn_all = _L1_gnn_setup()
    _L1_gnn_in = {k: v for k, v in _L1_gnn_all.items() if k in ('fc_w', 'fc_b', 'q_w', 'q_b', 'k_w', 'k_b', 'fp_w', 'fp_b')}
    del _L1_gnn_all
    return {'x': x, 'adj': adj, 'L0_gnn_W_q': _L0_gnn_in['W_q'], 'L0_gnn_W_k': _L0_gnn_in['W_k'], 'L0_gnn_W_v': _L0_gnn_in['W_v'], 'L0_gnn_W_e': _L0_gnn_in['W_e'], 'L0_gnn_W_o': _L0_gnn_in['W_o'], 'L1_gnn_fc_w': _L1_gnn_in['fc_w'], 'L1_gnn_fc_b': _L1_gnn_in['fc_b'], 'L1_gnn_q_w': _L1_gnn_in['q_w'], 'L1_gnn_q_b': _L1_gnn_in['q_b'], 'L1_gnn_k_w': _L1_gnn_in['k_w'], 'L1_gnn_k_b': _L1_gnn_in['k_b'], 'L1_gnn_fp_w': _L1_gnn_in['fp_w'], 'L1_gnn_fp_b': _L1_gnn_in['fp_b']}

def reference(x, adj, L0_gnn_W_q, L0_gnn_W_k, L0_gnn_W_v, L0_gnn_W_e, L0_gnn_W_o, L1_gnn_fc_w, L1_gnn_fc_b, L1_gnn_q_w, L1_gnn_q_b, L1_gnn_k_w, L1_gnn_k_b, L1_gnn_fp_w, L1_gnn_fp_b):
    import jax
    import jax.numpy as jnp

    def _L0_gnn_ref(h, edge, adj_mask, W_q, W_k, W_v, W_e, W_o):
        import math
        import jax, jax.numpy as jnp
        import numpy as np
        B, N, D, H = (32, 256, 128, 8)
        HD = D // H
        b, n, _ = h.shape
        q = (h @ W_q.T).reshape(b, n, H, HD).transpose(0, 2, 1, 3)
        k = (h @ W_k.T).reshape(b, n, H, HD).transpose(0, 2, 1, 3)
        v = (h @ W_v.T).reshape(b, n, H, HD).transpose(0, 2, 1, 3)
        edge_bias = jnp.einsum('bij,h->bhij', edge, W_e[:, 0])
        scores = jnp.einsum('bhid,bhjd->bhij', q, k) / math.sqrt(HD) + edge_bias
        scores = jnp.where(adj_mask[:, None], scores, -jnp.inf)
        attn = jax.nn.softmax(scores, axis=-1)
        out = jnp.einsum('bhij,bhjd->bhid', attn, v)
        out = out.transpose(0, 2, 1, 3).reshape(b, n, D)
        return out @ W_o.T

    def _L1_gnn_ref(feats, adj_mat, fc_w, fc_b, q_w, q_b, k_w, k_b, fp_w, fp_b):
        import jax, jax.numpy as jnp
        import numpy as np
        DIM = 128
        HEADS = 8
        BS = 8
        N = 512
        NEG = -1000000000.0
        bs, n, dim = feats.shape
        feat_proj = (feats @ fc_w + fc_b).reshape(bs, n, HEADS, dim).transpose(0, 2, 1, 3)
        q = feat_proj @ q_w + q_b
        k = feat_proj @ k_w + k_b
        logits = q + jnp.swapaxes(k, -1, -2)
        masked = logits + (1.0 - adj_mat[:, None]) * NEG
        masked = jax.nn.leaky_relu(masked, negative_slope=0.01)
        attn = jax.nn.softmax(masked, axis=-1)
        out = attn @ feat_proj
        out = out.transpose(0, 2, 1, 3).reshape(bs, n, HEADS * dim)
        out = out @ fp_w + fp_b + feats
        return jax.nn.sigmoid(out)
    x = _layernorm(x + _L0_gnn_ref(x, adj, adj, L0_gnn_W_q, L0_gnn_W_k, L0_gnn_W_v, L0_gnn_W_e, L0_gnn_W_o), axis=-1)
    x = _layernorm(x + _L1_gnn_ref(x, adj, L1_gnn_fc_w, L1_gnn_fc_b, L1_gnn_q_w, L1_gnn_q_b, L1_gnn_k_w, L1_gnn_k_b, L1_gnn_fp_w, L1_gnn_fp_b), axis=-1)
    return x

_drawn_inputs = setup_inputs


def setup_inputs(seed=0):
    import zlib

    import numpy as np

    out = dict(_drawn_inputs(seed))
    spreads = {'L1_gnn_fc_b': (0.0, 0.495), 'L1_gnn_fp_b': (0.0, 0.55)}
    factors = {}
    for name, (base, spread) in spreads.items():
        noise = np.random.default_rng([zlib.crc32(name.encode()), seed]).standard_normal(out[name].shape)
        drawn = base * np.exp(spread * noise) if base else spread * noise
        out[name] = jnp.asarray(drawn.astype(out[name].dtype))
    for name, factor in factors.items():
        out[name] = (out[name] * factor).astype(out[name].dtype)
    return out
```

```python
import concourse.bass as bass
from concourse import mybir
from contextlib import ExitStack


def gnn_kernel(nc, x, adj, W_q, W_k, W_v, W_e, W_o, fc_w, fc_b, q_w, q_b, k_w, k_b, fp_w, fp_b, out):
    fp32 = mybir.dt.float32
    i32 = mybir.dt.int32
    ALU = mybir.AluOpType
    ACT = mybir.ActivationFunctionType
    AX_X = mybir.AxisListType.X

    B, N, D = x.shape
    H = W_e.shape[0]
    HD = D // H
    P = 128
    NT = N // P
    HG = P // 32
    G = H // HG
    NEG = -1000000000.0
    MASKED = -3.0e38
    EPS = 1e-5

    ctx = ExitStack()
    with ctx:
        def sb(name, shape, dt=fp32):
            return ctx.enter_context(nc.sbuf_tensor(name, shape, dt))

        def sem(name):
            return ctx.enter_context(nc.semaphore(name))

        ident = sb("ident", [P, P])
        ones = sb("ones", [P, P])
        zeros = sb("zeros", [P, P])
        wq_rows = sb("wq_rows", [P, G, P])
        wk_rows = sb("wk_rows", [P, G, P])
        wv_rows = sb("wv_rows", [P, P])
        wo_rows = sb("wo_rows", [P, P])
        wqT = sb("wqT", [P, G, P])
        wkT = sb("wkT", [P, G, P])
        wvT = sb("wvT", [P, P])
        woT = sb("woT", [P, P])
        we = sb("we", [P, H])
        fcw = sb("fcw", [P, H * D])
        fcb = sb("fcb", [1, H * D])
        fpw = sb("fpw", [P, H, D])
        fpb = sb("fpb", [P, D])
        qw = sb("qw", [P, D])
        kw = sb("kw", [P, D])
        qkb = sb("qkb", [P, 2])
        flags = sb("flags", [1, B], i32)
        order = sb("order", [1, B], i32)

        gx = sb("gx", [P, NT, D])
        gadj = sb("gadj", [P, NT, N])
        gbias = sb("gbias", [P, NT, N])
        gxT = sb("gxT", [P, N])
        gq = sb("gq", [P, G, N])
        gk = sb("gk", [P, G, N])
        gv = sb("gv", [P, NT, D])
        gqt = sb("gqt", [P, G, P])
        gt = sb("gt", [P, N])
        gt2 = sb("gt2", [P, N])
        gmax = sb("gmax", [P, 1])
        gp = sb("gp", [P, N])
        gsum = sb("gsum", [P, 1])
        grec = sb("grec", [P, 1])
        gpT = sb("gpT", [P, NT, P])
        go = sb("go", [P, D])
        goT = sb("goT", [P, P])
        gx1 = sb("gx1", [P, NT, D])
        gy = sb("gy", [P, NT, D])
        gfp = sb("gfp", [P, NT, H * D])
        gprod = sb("gprod", [P, H, D])
        gql = sb("gql", [P, NT, H])
        gkl = sb("gkl", [P, NT, H])
        gqc = sb("gqc", [P, H])
        gdiag = sb("gdiag", [P, NT, P])
        gkrow = sb("gkrow", [P, H, N])
        gln = sb("gln", [P, D])
        gst = sb("gst", [P, 8])
        gstat = sb("gstat", [P, NT, 6])
        gmv = sb("gmv", [P, NT, 2])
        gvar = sb("gvar", [P, NT])
        grstd = sb("grstd", [P, NT])
        mhalf = sb("mhalf", [P, NT])
        gz = sb("gz", [P, D])

        bank = [ctx.enter_context(nc.psum_tensor(f"bank{i}", [P, 512], fp32)) for i in range(8)]

        s_load = sem("s_load")
        s_zero = sem("s_zero")
        s_ident0 = sem("s_ident0")
        s_ident = sem("s_ident")
        s_wT_ps = sem("s_wT_ps")
        s_wT = sem("s_wT")
        s_flags = sem("s_flags")

        g_in = sem("g_in")
        g_xT_ps = sem("g_xT_ps")
        g_xT = sem("g_xT")
        g_proj_ps = sem("g_proj_ps")
        g_proj = sem("g_proj")
        g_tile = sem("g_tile")
        g_score = [sem("g_score0")]
        g_max = [sem("g_max0"), sem("g_max1")]
        g_exp = [sem("g_exp0"), sem("g_exp1")]
        g_pT_ps = [sem("g_pT_ps0"), sem("g_pT_ps1")]
        g_pT = [sem("g_pT0"), sem("g_pT1")]
        g_o_ps = [sem("g_o_ps0"), sem("g_o_ps1")]
        g_o = [sem("g_o0"), sem("g_o1")]
        g_oT_ps = [sem("g_oT_ps0"), sem("g_oT_ps1")]
        g_oT = [sem("g_oT0"), sem("g_oT1")]
        g_y_ps = [sem("g_y_ps0"), sem("g_y_ps1")]
        g_x1 = sem("g_x1")
        g_x1T_ps = sem("g_x1T_ps")
        g_x1T = sem("g_x1T")
        g_fp_ps = sem("g_fp_ps")
        g_fp = sem("g_fp")
        g_diag = sem("g_diag")
        g_krow_ps = sem("g_krow_ps")
        g_krow = sem("g_krow")
        g_z = sem("g_z")
        g_sig = sem("g_sig")
        g_y = sem("g_y")
        g_var = [sem("g_var0"), sem("g_var1")]
        g_rstd = [sem("g_rstd0"), sem("g_rstd1")]
        g_out = sem("g_out")

        LOADS = 2 * H + 11
        def turn(eng, b):
            needed = eng.value_load(flags[0:1, bass.ds(b, 1)], min_val=0, max_val=1)
            before = eng.value_load(order[0:1, bass.ds(b, 1)], min_val=0, max_val=B - 1)
            return needed, before

        def general_sync(sp):
            with sp.Fori(0, B) as b:
                needed, k = turn(sp, b)
                f = k + 1
                with sp.If(needed > 0):
                    sp.dma_start(gx[:], x[bass.ds(b, 1)].rearrange("o (t p) d -> p (o t) d", p=P)).then_inc(g_in, 16)
                    sp.dma_start(gadj[:], adj[bass.ds(b, 1)].rearrange("o (t p) n -> p (o t) n", p=P)).then_inc(g_in, 16)
                    sp.wait_ge(g_y, f)
                    sp.dma_start(out[bass.ds(b, 1)].rearrange("o (t p) d -> p (o t) d", p=P), gy[:]).then_inc(g_out, 16)

        def general_scalar(act):
            with act.Fori(0, B) as b:
                needed, k = turn(act, b)
                f = k + 1
                with act.If(needed > 0):
                    for layer in (0, 1):
                        with act.Fori(0, NT) as it:
                            t = k * NT + it
                            for h in range(H):
                                r = t * H + h
                                act.wait_ge(g_max[layer], r + 1)
                                nc.scalar.activation(gp[:], gt2[:], ACT.Exp, bias=gmax[:, 0:1],
                                                     accum_out=gsum[:, 0:1]).then_inc(g_exp[layer], 1)
                            if layer:
                                act.wait_ge(g_z, t + 1)
                                nc.scalar.activation(gln[:], gz[:], ACT.Tanh, scale=0.5).then_inc(g_sig, 1)

        def layernorm(dve, dst, src, layer, f):
            for t in range(NT):
                nc.vector.bn_stats(gstat[:, t, :], src[:, t, :])
            dve.drain()
            for t in range(NT):
                nc.vector.bn_aggr(gmv[:, t, :], gstat[:, t, :])
            dve.drain()
            nc.vector.tensor_scalar(gvar[:], gmv[:, :, 1], EPS, None, ALU.add).then_inc(g_var[layer], 1)
            dve.wait_ge(g_rstd[layer], f)
            for t in range(NT):
                last = nc.vector.tensor_scalar(dst[:, t, :], src[:, t, :], gmv[:, t, 0:1], grstd[:, t:t + 1],
                                               ALU.subtract, ALU.mult)
            return last

        def general_gpsimd(pool):
            with pool.Fori(0, B) as b:
                needed, k = turn(pool, b)
                f = k + 1
                with pool.If(needed > 0):
                    for layer in (0, 1):
                        pool.wait_ge(g_var[layer], f)
                        nc.gpsimd.tensor_tensor(grstd[:], gvar[:], mhalf[:], ALU.pow).then_inc(g_rstd[layer], 1)

        def general_vector(dve):
            flat = lambda m: m[:].rearrange("p t n -> p (t n)")
            with dve.Fori(0, B) as b:
                needed, k = turn(dve, b)
                f = k + 1
                with dve.If(needed > 0):
                    dve.wait_ge(s_load, 16 * LOADS)
                    dve.wait_ge(g_in, f * 32)
                    nc.vector.tensor_scalar(flat(gbias), flat(gadj), 0.0, MASKED, ALU.is_equal, ALU.mult)
                    dve.wait_ge(g_xT_ps, f)
                    nc.vector.tensor_copy(gxT[:], bank[0][:]).then_inc(g_xT, 1)
                    dve.wait_ge(g_proj_ps, f)
                    for g in range(G):
                        nc.vector.tensor_copy(gq[:, g, :], bank[1 + g][:])
                        nc.vector.tensor_copy(gk[:, g, :], bank[1 + G + g][:])
                    nc.vector.tensor_copy(flat(gv), bank[1 + 2 * G][:]).then_inc(g_proj, 1)
                    dve.drain()
                    with dve.Fori(0, NT) as it:
                        t = k * NT + it
                        for g in range(G):
                            last = nc.vector.tensor_copy(gqt[:, g, :], gq[:, g, bass.ds(it * P, P)])
                        last.then_inc(g_tile, 1)
                        for h in range(H):
                            r = t * H + h
                            dve.wait_ge(g_score[0], r + 1)
                            nc.vector.scalar_tensor_tensor(gt[:], flat(gadj)[:, bass.ds(it * N, N)], we[:, h:h + 1],
                                                           bank[0][:], ALU.mult, ALU.add)
                            dve.drain()
                            nc.vector.tensor_tensor(gt2[:], gt[:], flat(gbias)[:, bass.ds(it * N, N)], ALU.add)
                            dve.drain()
                            head(dve, 0, r, go[:, h * HD:(h + 1) * HD], bank[3][:, h * HD:(h + 1) * HD])
                        dve.drain()
                        nc.vector.tensor_copy(gst[:, 0:1], grec[:]).then_inc(g_o[0], 1)
                        dve.wait_ge(g_oT_ps[0], t + 1)
                        nc.vector.tensor_copy(goT[:], bank[5][:, 0:P]).then_inc(g_oT[0], 1)
                        dve.wait_ge(g_y_ps[0], t + 1)
                        nc.vector.tensor_tensor(flat(gy)[:, bass.ds(it * D, D)], bank[4][:, 0:D],
                                                flat(gx)[:, bass.ds(it * D, D)], ALU.add)
                    dve.drain()
                    layernorm(dve, gx1, gy, 0, f).then_inc(g_x1, 1)
                    nc.vector.tensor_scalar(flat(gbias), flat(gadj), -1.0, 1.0, ALU.mult, ALU.add)
                    dve.drain()
                    nc.vector.tensor_scalar(flat(gbias), flat(gbias), NEG, None, ALU.mult)
                    dve.wait_ge(g_x1T_ps, f)
                    nc.vector.tensor_copy(gxT[:], bank[0][:]).then_inc(g_x1T, 1)
                    for jt in range(NT):
                        dve.wait_ge(g_fp_ps, k * NT + jt + 1)
                        nc.vector.tensor_copy(gfp[:, jt, 0:512], bank[1][:])
                        nc.vector.tensor_copy(gfp[:, jt, 512:1024], bank[2][:]).then_inc(g_fp, 1)
                        dve.drain()
                        fp3 = gfp[:, jt, :].rearrange("p (h d) -> p h d", h=H)
                        for w, dst, n in ((qw, gql, 0), (kw, gkl, 1)):
                            for h in range(H):
                                nc.vector.tensor_tensor(gprod[:, h, :], fp3[:, h, :], w[:], ALU.mult)
                            dve.drain()
                            nc.vector.tensor_reduce(dst[:, jt, :], gprod[:], AX_X, ALU.add)
                            dve.drain()
                            nc.vector.tensor_scalar(dst[:, jt, :], dst[:, jt, :], qkb[:, n:n + 1], None, ALU.add)
                    dve.drain()
                    for h in range(H):
                        for jt in range(NT):
                            last = nc.vector.tensor_scalar(gdiag[:, jt, :], ident[:], gkl[:, jt, h:h + 1], None, ALU.mult)
                        last.then_inc(g_diag, 1)
                        dve.wait_ge(g_krow_ps, k * H + h + 1)
                        nc.vector.tensor_copy(gkrow[:, h, :], bank[3][:]).then_inc(g_krow, 1)
                    dve.drain()
                    with dve.Fori(0, NT) as it:
                        t = k * NT + it
                        nc.vector.tensor_copy(gqc[:], flat(gql)[:, bass.ds(it * H, H)])
                        dve.drain()
                        for h in range(H):
                            r = t * H + h
                            nc.vector.scalar_tensor_tensor(gt[:], gkrow[:, h, :], gqc[:, h:h + 1],
                                                           flat(gbias)[:, bass.ds(it * N, N)], ALU.add, ALU.add)
                            dve.drain()
                            nc.vector.scalar_tensor_tensor(gt2[:], gt[:], 0.01, gt[:], ALU.mult, ALU.max)
                            dve.drain()
                            head(dve, 1, r, go[:], bank[3][:, 0:D])
                            dve.drain()
                            nc.vector.tensor_copy(gst[:, 0:1], grec[:]).then_inc(g_o[1], 1)
                            dve.wait_ge(g_oT_ps[1], r + 1)
                            nc.vector.tensor_copy(goT[:], bank[5][:, 0:P]).then_inc(g_oT[1], 1)
                        dve.wait_ge(g_y_ps[1], t + 1)
                        nc.vector.tensor_tensor(gz[:], bank[4][:, 0:D], fpb[:], ALU.add)
                        dve.drain()
                        nc.vector.tensor_tensor(gz[:], gz[:], flat(gx1)[:, bass.ds(it * D, D)], ALU.add).then_inc(g_z, 1)
                        dve.wait_ge(g_sig, t + 1)
                        nc.vector.tensor_scalar(gz[:], gln[:], 0.5, 0.5, ALU.mult, ALU.add)
                        dve.drain()
                        nc.vector.tensor_tensor(flat(gx)[:, bass.ds(it * D, D)], gz[:],
                                                flat(gx1)[:, bass.ds(it * D, D)], ALU.add)
                        dve.drain()
                    layernorm(dve, gy, gx, 1, f).then_inc(g_y, 1)

        def head(dve, layer, r, dst, o_ps):
            nc.vector.tensor_reduce(gst[:, 0:1], gt2[:], AX_X, ALU.max)
            dve.drain()
            nc.vector.tensor_scalar(gmax[:], gst[:, 0:1], -1.0, None, ALU.mult).then_inc(g_max[layer], 1)
            dve.wait_ge(g_exp[layer], r + 1)
            nc.vector.reciprocal(grec[:], gsum[:])
            dve.wait_ge(g_pT_ps[layer], r + 1)
            nc.vector.tensor_copy(gpT[:].rearrange("p t n -> p (t n)"), bank[2][:]).then_inc(g_pT[layer], 1)
            dve.wait_ge(g_o_ps[layer], r + 1)
            nc.vector.tensor_scalar(dst, o_ps, grec[:, 0:1], None, ALU.mult)

        def general_tensor(pe):
            def mm(o, l, r, start=True, stop=True):
                return nc.tensor.matmul(o, l, r, start=start, stop=stop)

            with pe.Fori(0, B) as b:
                needed, k = turn(pe, b)
                f = k + 1
                with pe.If(needed > 0):
                    pe.wait_ge(g_in, f * 32)
                    for t in range(NT):
                        last = nc.tensor.transpose(bank[0][:, t * P:(t + 1) * P], gx[:, t, :], ident[:])
                    last.then_inc(g_xT_ps, 1)
                    pe.wait_ge(g_xT, f)
                    for g in range(G):
                        mm(bank[1 + g][:], wqT[:, g, :], gxT[:])
                        mm(bank[1 + G + g][:], wkT[:, g, :], gxT[:])
                    for t in range(NT):
                        last = mm(bank[1 + 2 * G][:, t * P:(t + 1) * P], gxT[:, t * P:(t + 1) * P], wvT[:])
                    last.then_inc(g_proj_ps, 1)
                    with pe.Fori(0, NT) as it:
                        t = k * NT + it
                        pe.wait_ge(g_proj, f)
                        pe.wait_ge(g_tile, t + 1)
                        for h in range(H):
                            r = t * H + h
                            c = 32 * (h % HG)
                            mm(bank[0][:], gqt[c:c + 32, h // HG, :], gk[c:c + 32, h // HG, :]).then_inc(g_score[0], 1)
                            pe.wait_ge(g_exp[0], r + 1)
                            for j in range(NT):
                                last = nc.tensor.transpose(bank[2][:, j * P:(j + 1) * P], gp[:, j * P:(j + 1) * P], ident[:])
                            last.then_inc(g_pT_ps[0], 1)
                            pe.wait_ge(g_pT[0], r + 1)
                            for j in range(NT):
                                last = mm(bank[3][:, h * HD:(h + 1) * HD], gpT[:, j, :], gv[:, j, h * HD:(h + 1) * HD],
                                          j == 0, j == NT - 1)
                            last.then_inc(g_o_ps[0], 1)
                        pe.wait_ge(g_o[0], t + 1)
                        nc.tensor.transpose(bank[5][:, 0:P], go[:], ident[:]).then_inc(g_oT_ps[0], 1)
                        pe.wait_ge(g_oT[0], t + 1)
                        mm(bank[4][:, 0:D], goT[:], woT[:]).then_inc(g_y_ps[0], 1)
                    pe.wait_ge(g_x1, f)
                    for t in range(NT):
                        last = nc.tensor.transpose(bank[0][:, t * P:(t + 1) * P], gx1[:, t, :], ident[:])
                    last.then_inc(g_x1T_ps, 1)
                    pe.wait_ge(g_x1T, f)
                    for jt in range(NT):
                        if jt:
                            pe.wait_ge(g_fp, k * NT + jt)
                        for half in range(2):
                            cols = slice(half * 512, half * 512 + 512)
                            mm(bank[1 + half][:], gxT[:, jt * P:(jt + 1) * P], fcw[:, cols], True, False)
                            last = mm(bank[1 + half][:], ones[0:1, :], fcb[0:1, cols], False, True)
                        last.then_inc(g_fp_ps, 1)
                    for h in range(H):
                        pe.wait_ge(g_diag, k * H + h + 1)
                        if h:
                            pe.wait_ge(g_krow, k * H + h)
                        mm(bank[3][:], ones[:], gdiag[:].rearrange("p t n -> p (t n)")).then_inc(g_krow_ps, 1)
                    with pe.Fori(0, NT) as it:
                        t = k * NT + it
                        for h in range(H):
                            r = t * H + h
                            pe.wait_ge(g_exp[1], r + 1)
                            for j in range(NT):
                                last = nc.tensor.transpose(bank[2][:, j * P:(j + 1) * P], gp[:, j * P:(j + 1) * P], ident[:])
                            last.then_inc(g_pT_ps[1], 1)
                            pe.wait_ge(g_pT[1], r + 1)
                            for j in range(NT):
                                last = mm(bank[3][:, 0:D], gpT[:, j, :], gfp[:, j, h * D:(h + 1) * D], j == 0, j == NT - 1)
                            last.then_inc(g_o_ps[1], 1)
                            pe.wait_ge(g_o[1], r + 1)
                            nc.tensor.transpose(bank[5][:, 0:P], go[:], ident[:]).then_inc(g_oT_ps[1], 1)
                            pe.wait_ge(g_oT[1], r + 1)
                            last = mm(bank[4][:, 0:D], goT[:], fpw[:, h, :], h == 0, h == H - 1)
                        last.then_inc(g_y_ps[1], 1)
                    pe.wait_ge(g_out, f * 16)


        block = ctx.enter_context(nc.Block())

        @block.sync
        def _(sp):
            sp.wait_ge(s_zero, 2)
            for rows, w in ((wq_rows, W_q), (wk_rows, W_k)):
                for h in range(H):
                    sp.dma_start(rows[32 * (h % HG):32 * (h % HG) + HD, h // HG, :],
                                 w[h * HD:(h + 1) * HD, :]).then_inc(s_load, 16)
            sp.dma_start(wv_rows[:], W_v).then_inc(s_load, 16)
            sp.dma_start(wo_rows[:], W_o).then_inc(s_load, 16)
            sp.dma_start(we[:], W_e.rearrange("h o -> o h").to_broadcast([P, H])).then_inc(s_load, 16)
            sp.dma_start(fcw[:], fc_w).then_inc(s_load, 16)
            sp.dma_start(fcb[:], fc_b.rearrange("(o n) -> o n", o=1)).then_inc(s_load, 16)
            sp.dma_start(fpw[:], fp_w.rearrange("(h c) n -> c h n", h=H)).then_inc(s_load, 16)
            sp.dma_start(fpb[:], fp_b.rearrange("(o n) -> o n", o=1).to_broadcast([P, D])).then_inc(s_load, 16)
            sp.dma_start(qw[:], q_w.rearrange("n o -> o n").to_broadcast([P, D])).then_inc(s_load, 16)
            sp.dma_start(kw[:], k_w.rearrange("n o -> o n").to_broadcast([P, D])).then_inc(s_load, 16)
            sp.dma_start(qkb[:, 0:1], q_b.rearrange("(o n) -> o n", o=1).to_broadcast([P, 1])).then_inc(s_load, 16)
            sp.dma_start(qkb[:, 1:2], k_b.rearrange("(o n) -> o n", o=1).to_broadcast([P, 1])).then_inc(s_load, 16)
            sp.wait_ge(s_flags, 1)
            general_sync(sp)

        @block.gpsimd
        def _(pool):
            pool.memset(wq_rows[:], 0.0).then_inc(s_zero, 1)
            pool.memset(wk_rows[:], 0.0).then_inc(s_zero, 1)
            pool.memset(zeros[:], 0.0).then_inc(s_ident0, 1)
            pool.memset(ones[:], 1.0).then_inc(s_ident, 1)
            pool.wait_ge(s_ident0, 1)
            pool.affine_select(out=ident[:], in_=zeros[:], compare_op=ALU.not_equal, fill=1.0, base=0,
                               pattern=[[-1, P]], channel_multiplier=1).then_inc(s_ident, 1)
            pool.memset(mhalf[:], -0.5).then_inc(s_ident, 1)
            pool.wait_ge(s_flags, 1)
            pool.wait_ge(s_ident, 3)
            general_gpsimd(pool)

        @block.scalar
        def _(act):
            act.wait_ge(s_flags, 1)
            general_scalar(act)

        @block.vector
        def _(dve):
            dve.wait_ge(s_wT_ps, 1)
            nc.vector.tensor_scalar(wqT[:].rearrange("p g n -> p (g n)"), bank[0][:, 0:G * P],
                                    float(HD) ** -0.5, None, ALU.mult)
            nc.vector.tensor_copy(wkT[:].rearrange("p g n -> p (g n)"), bank[1][:, 0:G * P])
            nc.vector.tensor_copy(wvT[:], bank[2][:, 0:P])
            nc.vector.tensor_copy(woT[:], bank[3][:, 0:P]).then_inc(s_wT, 1)
            dve.wait_ge(s_ident, 3)
            for b in range(B):
                nc.vector.memset(flags[:, b:b + 1], 1)
                nc.vector.memset(order[:, b:b + 1], b)
            dve.drain()
            nc.vector.tensor_copy(gmax[:], ones[:, 0:1]).then_inc(s_flags, 1)
            general_vector(dve)

        @block.tensor
        def _(pe):
            pe.wait_ge(s_ident, 2)
            pe.wait_ge(s_load, 16 * LOADS)
            for g in range(G):
                nc.tensor.transpose(bank[0][:, g * P:(g + 1) * P], wq_rows[:, g, :], ident[:])
                nc.tensor.transpose(bank[1][:, g * P:(g + 1) * P], wk_rows[:, g, :], ident[:])
            nc.tensor.transpose(bank[2][:, 0:P], wv_rows[:], ident[:])
            nc.tensor.transpose(bank[3][:, 0:P], wo_rows[:], ident[:]).then_inc(s_wT_ps, 1)
            pe.wait_ge(s_wT, 1)
            pe.wait_ge(s_flags, 1)
            general_tensor(pe)


_INS = ['x', 'adj', 'L0_gnn_W_q', 'L0_gnn_W_k', 'L0_gnn_W_v', 'L0_gnn_W_e', 'L0_gnn_W_o', 'L1_gnn_fc_w', 'L1_gnn_fc_b',
        'L1_gnn_q_w', 'L1_gnn_q_b', 'L1_gnn_k_w', 'L1_gnn_k_b', 'L1_gnn_fp_w', 'L1_gnn_fp_b']


def kernel(**inputs):
    import numpy as _np
    import concourse.bacc as _bacc
    from concourse import mybir as _mybir
    from concourse.bass_utils import run_bass_kernel_spmd as _run

    nc = _bacc.Bacc("TRN2", target_bir_lowering=False, num_devices=1)
    arrays, args = {}, []
    for name in _INS:
        a = _np.ascontiguousarray(inputs[name])
        arrays[f"in_{name}_dram"] = a
        args.append(nc.dram_tensor(f"in_{name}_dram", a.shape, _mybir.dt.from_np(a.dtype), kind="ExternalInput").ap())
    o = nc.dram_tensor("out_0_dram", inputs["x"].shape, _mybir.dt.float32, kind="ExternalOutput").ap()
    gnn_kernel(nc, *args, o)
    r = _run(nc, [arrays], core_ids=[0])
    return r.results[0]["out_0_dram"]
```

```python
import concourse.bass as bass
from concourse import mybir
from contextlib import ExitStack


def gnn_kernel(nc, x, adj, W_q, W_k, W_v, W_e, W_o, fc_w, fc_b, q_w, q_b, k_w, k_b, fp_w, fp_b, out):
    fp32 = mybir.dt.float32
    bf16 = mybir.dt.bfloat16
    i32 = mybir.dt.int32
    ALU = mybir.AluOpType
    ACT = mybir.ActivationFunctionType
    AX_X = mybir.AxisListType.X

    B, N, D = x.shape
    H = W_e.shape[0]
    HD = D // H
    P = 128
    NT = N // P
    HG = P // 32
    G = H // HG
    NEG = -1000000000.0
    MASKED = -3.0e38
    BIG = 1.0e30
    EPS = 1e-5

    ctx = ExitStack()
    with ctx:
        def sb(name, shape, dt=fp32):
            return ctx.enter_context(nc.sbuf_tensor(name, shape, dt))

        def sem(name):
            return ctx.enter_context(nc.semaphore(name))

        HALF = 2 * H
        PARTS = ((0, 0), (0, 1), (1, 0), (1, 1), (0, 2), (2, 0))
        KR = HD * len(PARTS)

        ident = sb("ident", [P, P])
        identb = sb("identb", [P, P], bf16)
        ones = sb("ones", [P, P])
        tri = sb("tri", [B, 2 * B])
        mhalf = sb("mhalf", [P, 2 * H])
        phalf = sb("phalf", [P, 2 * H])
        wqT = sb("wqT", [P, P])
        wkT = sb("wkT", [P, P])
        wvT = sb("wvT", [P, P])
        woT = sb("woT", [P, P])
        wqTg = sb("wqTg", [P, G, P])
        wkTg = sb("wkTg", [P, G, P])
        we = sb("we", [P, H])
        fcw = sb("fcw", [P, H * D])
        fcb = sb("fcb", [1, H * D])
        fpw = sb("fpw", [P, H, D])
        fpb = sb("fpb", [P, D])
        wf = sb("wf", [P, D])
        bf = sb("bf", [P, D])
        qw = sb("qw", [P, D])
        kw = sb("kw", [P, D])
        qkcol = sb("qkcol", [P, 2])
        qkb = sb("qkb", [P, 2])
        sgn = sb("sgn", [1, 2 * H], i32)
        gapmin = sb("gapmin", [P, 1])
        wesq = sb("wesq", [P, H])
        checks = sb("checks", [P, B])
        flags = sb("flags", [1, 2 * B], i32)
        fcol = sb("fcol", [B, 1])
        weok = sb("weok", [P, 1])
        nsq = sb("nsq", [P, 4 * H])
        nrm = sb("nrm", [P, 2 * H])
        nab = sb("nab", [P, 2 * H])
        fcb8 = sb("fcb8", [H, D])
        fcbT = sb("fcbT", [P, H])
        order = flags[0:1, B:2 * B]

        X = sb("X", [P, NT, D])
        XR = sb("XR", [P, NT, D])
        A = [sb(f"A{i}", [P, NT, N]) for i in range(2)]
        AT = [sb(f"AT{i}", [P, 2, NT, N]) for i in range(2)]
        MT = sb("MT", [P, NT, N])
        QK = [sb(f"QK{i}", [P, 2, H, N], bf16) for i in range(2)]
        SPL = sb("SPL", [P, 2, 3, N], bf16)
        RES = sb("RES", [P, 2, N])
        V = [sb(f"V{i}", [P, NT, H, 32]) for i in range(2)]
        TE = [sb(f"TE{i}", [P, 2, N]) for i in range(4)]
        XT = sb("XT", [P, N])
        MX = [sb(f"MX{i}", [P, NT, 8]) for i in range(2)]
        OH = sb("OH", [P, NT, N], bf16)
        PT = [sb(f"PT{i}", [P, NT, N], bf16) for i in range(2)]
        OS = sb("OS", [P, G, N])
        RD = [sb(f"RD{i}", [P, G, NT, HG]) for i in range(2)]
        ON = sb("ON", [P, NT, H, HD])
        ONT = sb("ONT", [P, N])
        Y = sb("Y", [P, NT, D])
        ST = sb("ST", [P, NT, 6])
        MV = sb("MV", [P, 2, NT, 2])
        VAR = sb("VAR", [P, 2, NT])
        RS = sb("RS", [P, 2, NT])
        NM = sb("NM", [P, 2, NT])
        X1 = sb("X1", [P, NT, D])
        CS = sb("CS", [P, 3, NT, D], bf16)
        CR = sb("CR", [P, NT, D])
        XB = sb("XB", [P, NT, D])
        XH = sb("XH", [P, NT, D])
        GT = sb("GT", [P, N])
        Z = sb("Z", [P, NT, D])
        TH = sb("TH", [P, NT, D])
        U = sb("U", [P, NT, D])
        OUT = sb("OUT", [P, NT, D])
        CK = sb("CK", [P, 4, 2 * NT])
        CD = sb("CD", [P, 3, G * NT * HG])

        wq_rows, wk_rows, wv_rows, wo_rows = (A[1][:, 0, i * P:(i + 1) * P] for i in range(4))
        fcT = A[1][:, 1:3, :].rearrange("p t n -> p (t n)").rearrange("p (h d) -> p h d", h=H)
        fcB = AT[1][:, 0, 0:2, :].rearrange("p t n -> p (t n)").rearrange("p (h d) -> p h d", h=H)
        prod = AT[1][:, 1, 0:2, :].rearrange("p t n -> p (t n)").rearrange("p (h d) -> p h d", h=H)

        gx = X
        gadj = A[0]
        gbias = A[1]
        gxT = XT
        qkf = QK[0][:].rearrange("p a h n -> p (a h n)").bitcast(fp32)
        gq = qkf[:, 0:G * N].rearrange("p (g n) -> p g n", g=G)
        gk = qkf[:, G * N:2 * G * N].rearrange("p (g n) -> p g n", g=G)
        gqt = qkf[:, 2 * G * N:2 * G * N + G * P].rearrange("p (g n) -> p g n", g=G)
        gv = Y
        gt = TE[0][:, 0, :]
        gt2 = TE[0][:, 1, :]
        gmax = sb("gmax", [P, 1])
        gp = TE[1][:, 0, :]
        gsum = sb("gsum", [P, 1])
        grec = sb("grec", [P, 1])
        gpT = CR
        go = sb("go", [P, D])
        goT = sb("goT", [P, P])
        gx1 = X1
        gy = OUT
        gfp = AT[0][:].rearrange("p a t n -> p (a t n)").rearrange("p (t n) -> p t n", t=NT)
        gkrow = AT[1][:].rearrange("p a t n -> p (a t) n")
        gprod = TE[2][:].rearrange("p a n -> p (a n)").rearrange("p (h d) -> p h d", h=H)
        gql = sb("gql", [P, NT, H])
        gkl = sb("gkl", [P, NT, H])
        gqc = sb("gqc", [P, H])
        gdiag = Z
        gln = sb("gln", [P, D])
        gst = sb("gst", [P, 8])
        gstat = ST
        gmv = sb("gmv", [P, NT, 2])
        gvar = sb("gvar", [P, NT])
        grstd = sb("grstd", [P, NT])
        gz = sb("gz", [P, D])

        scratch = nc.dram_tensor("qk_parts", (2, P, 2, 3, N), bf16, kind="Internal").ap()

        bank = [ctx.enter_context(nc.psum_tensor(f"bank{i}", [P, 512], fp32)) for i in range(8)]
        S_BANK, O_BANK, M_BANK = bank[0:4], bank[4:6], bank[6:8]

        s_w = sem("s_w")
        s_c = sem("s_c")
        s_wT_ps = sem("s_wT_ps")
        s_wT = sem("s_wT")
        s_fold_ps = sem("s_fold_ps")
        s_fold_in = sem("s_fold_in")
        s_const = sem("s_const")
        s_norm = sem("s_norm")
        s_root = sem("s_root")
        s_vones = sem("s_vones")
        s_bad = sem("s_bad")
        s_cnt_ps = sem("s_cnt_ps")
        s_cnt = sem("s_cnt")
        s_ord_ps = sem("s_ord_ps")
        s_flags = sem("s_flags")

        x_in = sem("x_in")
        a_in = sem("a_in")
        xr_in = sem("xr_in")
        spl_out = sem("spl_out")
        stack_in = sem("stack_in")
        out_st = sem("out_st")
        p_full = sem("p_full")
        p_act = sem("p_act")
        p_dve = sem("p_dve")
        p_pool = sem("p_pool")
        qk_ready = sem("qk_ready")
        biased = sem("biased")
        exped = sem("exped")
        pv_done = sem("pv_done")
        onehot = sem("onehot")
        maxed = sem("maxed")
        m_full = sem("m_full")
        m_act = sem("m_act")
        recip = sem("recip")
        normed = sem("normed")
        t_full = sem("t_full")
        t_act = sem("t_act")
        t_y = sem("t_y")
        t_z = sem("t_z")
        t_u = sem("t_u")
        t_mv = sem("t_mv")
        t_rs = sem("t_rs")
        t_x1 = sem("t_x1")
        t_cs = sem("t_cs")
        t_xb = sem("t_xb")
        t_out = sem("t_out")
        t_ck = sem("t_ck")

        g_in = sem("g_in")
        g_xT_ps = sem("g_xT_ps")
        g_xT = sem("g_xT")
        g_proj_ps = sem("g_proj_ps")
        g_proj = sem("g_proj")
        g_tile = sem("g_tile")
        g_score = [sem("g_score0")]
        g_max = [sem("g_max0"), sem("g_max1")]
        g_exp = [sem("g_exp0"), sem("g_exp1")]
        g_pT_ps = [sem("g_pT_ps0"), sem("g_pT_ps1")]
        g_pT = [sem("g_pT0"), sem("g_pT1")]
        g_o_ps = [sem("g_o_ps0"), sem("g_o_ps1")]
        g_o = [sem("g_o0"), sem("g_o1")]
        g_oT_ps = [sem("g_oT_ps0"), sem("g_oT_ps1")]
        g_oT = [sem("g_oT0"), sem("g_oT1")]
        g_y_ps = [sem("g_y_ps0"), sem("g_y_ps1")]
        g_x1 = sem("g_x1")
        g_x1T_ps = sem("g_x1T_ps")
        g_x1T = sem("g_x1T")
        g_fp_ps = sem("g_fp_ps")
        g_fp = sem("g_fp")
        g_diag = sem("g_diag")
        g_krow_ps = sem("g_krow_ps")
        g_krow = sem("g_krow")
        g_z = sem("g_z")
        g_sig = sem("g_sig")
        g_y = sem("g_y")
        g_var = [sem("g_var0"), sem("g_var1")]
        g_rstd = [sem("g_rstd0"), sem("g_rstd1")]
        g_out = sem("g_out")

        WEIGHT_LOADS = 16
        nc.disable_value_cache = True
        signs = []

        def turn(eng, b):
            needed = eng.value_load(flags[0:1, bass.ds(b, 1)], min_val=0, max_val=1)
            before = eng.value_load(order[0:1, bass.ds(b, 1)], min_val=0, max_val=B - 1)
            return needed, before

        def general_sync(sp):
            with sp.Fori(0, B) as b:
                needed, k = turn(sp, b)
                f = k + 1
                with sp.If(needed > 0):
                    sp.dma_start(gx[:], x[bass.ds(b, 1)].rearrange("o (t p) d -> p (o t) d", p=P)).then_inc(g_in, 16)
                    sp.dma_start(gadj[:], adj[bass.ds(b, 1)].rearrange("o (t p) n -> p (o t) n", p=P)).then_inc(g_in, 16)
                    sp.wait_ge(g_y, f)
                    sp.dma_start(out[bass.ds(b, 1)].rearrange("o (t p) d -> p (o t) d", p=P), gy[:]).then_inc(g_out, 16)

        def general_scalar(act):
            with act.Fori(0, B) as b:
                needed, k = turn(act, b)
                f = k + 1
                with act.If(needed > 0):
                    for layer in (0, 1):
                        with act.Fori(0, NT) as it:
                            t = k * NT + it
                            for h in range(H):
                                r = t * H + h
                                act.wait_ge(g_max[layer], r + 1)
                                nc.scalar.activation(gp[:], gt2[:], ACT.Exp, bias=gmax[:, 0:1],
                                                     accum_out=gsum[:, 0:1]).then_inc(g_exp[layer], 1)
                            if layer:
                                act.wait_ge(g_z, t + 1)
                                nc.scalar.activation(gln[:], gz[:], ACT.Tanh, scale=0.5).then_inc(g_sig, 1)

        def layernorm(dve, dst, src, layer, f):
            for t in range(NT):
                nc.vector.bn_stats(gstat[:, t, :], src[:, t, :])
            dve.drain()
            for t in range(NT):
                nc.vector.bn_aggr(gmv[:, t, :], gstat[:, t, :])
            dve.drain()
            nc.vector.tensor_scalar(gvar[:], gmv[:, :, 1], EPS, None, ALU.add).then_inc(g_var[layer], 1)
            dve.wait_ge(g_rstd[layer], f)
            for t in range(NT):
                last = nc.vector.tensor_scalar(dst[:, t, :], src[:, t, :], gmv[:, t, 0:1], grstd[:, t:t + 1],
                                               ALU.subtract, ALU.mult)
            return last

        def general_gpsimd(pool):
            with pool.Fori(0, B) as b:
                needed, k = turn(pool, b)
                f = k + 1
                with pool.If(needed > 0):
                    for layer in (0, 1):
                        pool.wait_ge(g_var[layer], f)
                        nc.gpsimd.tensor_tensor(grstd[:], gvar[:], mhalf[:, 0:NT], ALU.pow).then_inc(g_rstd[layer], 1)

        def general_vector(dve):
            flat = lambda m: m[:].rearrange("p t n -> p (t n)")
            with dve.Fori(0, B) as b:
                needed, k = turn(dve, b)
                f = k + 1
                with dve.If(needed > 0):
                    dve.wait_ge(g_in, f * 32)
                    nc.vector.tensor_scalar(flat(gbias), flat(gadj), 0.0, MASKED, ALU.is_equal, ALU.mult)
                    dve.wait_ge(g_xT_ps, f)
                    nc.vector.tensor_copy(gxT[:], bank[0][:]).then_inc(g_xT, 1)
                    dve.wait_ge(g_proj_ps, f)
                    for g in range(G):
                        nc.vector.tensor_copy(gq[:, g, :], bank[1 + g][:])
                        nc.vector.tensor_copy(gk[:, g, :], bank[1 + G + g][:])
                    nc.vector.tensor_copy(flat(gv), bank[1 + 2 * G][:]).then_inc(g_proj, 1)
                    dve.drain()
                    with dve.Fori(0, NT) as it:
                        t = k * NT + it
                        for g in range(G):
                            last = nc.vector.tensor_copy(gqt[:, g, :], gq[:, g, bass.ds(it * P, P)])
                        last.then_inc(g_tile, 1)
                        for h in range(H):
                            r = t * H + h
                            dve.wait_ge(g_score[0], r + 1)
                            nc.vector.scalar_tensor_tensor(gt[:], flat(gadj)[:, bass.ds(it * N, N)], we[:, h:h + 1],
                                                           bank[0][:], ALU.mult, ALU.add)
                            dve.drain()
                            nc.vector.tensor_tensor(gt2[:], gt[:], flat(gbias)[:, bass.ds(it * N, N)], ALU.add)
                            dve.drain()
                            head(dve, 0, r, go[:, h * HD:(h + 1) * HD], bank[3][:, h * HD:(h + 1) * HD])
                        dve.drain()
                        nc.vector.tensor_copy(gst[:, 0:1], grec[:]).then_inc(g_o[0], 1)
                        dve.wait_ge(g_oT_ps[0], t + 1)
                        nc.vector.tensor_copy(goT[:], bank[5][:, 0:P]).then_inc(g_oT[0], 1)
                        dve.wait_ge(g_y_ps[0], t + 1)
                        nc.vector.tensor_tensor(flat(gy)[:, bass.ds(it * D, D)], bank[4][:, 0:D],
                                                flat(gx)[:, bass.ds(it * D, D)], ALU.add)
                    dve.drain()
                    layernorm(dve, gx1, gy, 0, f).then_inc(g_x1, 1)
                    nc.vector.tensor_scalar(flat(gbias), flat(gadj), -1.0, 1.0, ALU.mult, ALU.add)
                    dve.drain()
                    nc.vector.tensor_scalar(flat(gbias), flat(gbias), NEG, None, ALU.mult)
                    dve.wait_ge(g_x1T_ps, f)
                    nc.vector.tensor_copy(gxT[:], bank[0][:]).then_inc(g_x1T, 1)
                    for jt in range(NT):
                        dve.wait_ge(g_fp_ps, k * NT + jt + 1)
                        nc.vector.tensor_copy(gfp[:, jt, 0:512], bank[1][:])
                        nc.vector.tensor_copy(gfp[:, jt, 512:1024], bank[2][:]).then_inc(g_fp, 1)
                        dve.drain()
                        fp3 = gfp[:, jt, :].rearrange("p (h d) -> p h d", h=H)
                        for w, dst, n in ((qw, gql, 0), (kw, gkl, 1)):
                            for h in range(H):
                                nc.vector.tensor_tensor(gprod[:, h, :], fp3[:, h, :], w[:], ALU.mult)
                            dve.drain()
                            nc.vector.tensor_reduce(dst[:, jt, :], gprod[:], AX_X, ALU.add)
                            dve.drain()
                            nc.vector.tensor_scalar(dst[:, jt, :], dst[:, jt, :], qkb[:, n:n + 1], None, ALU.add)
                    dve.drain()
                    for h in range(H):
                        for jt in range(NT):
                            last = nc.vector.tensor_scalar(gdiag[:, jt, :], ident[:], gkl[:, jt, h:h + 1], None, ALU.mult)
                        last.then_inc(g_diag, 1)
                        dve.wait_ge(g_krow_ps, k * H + h + 1)
                        nc.vector.tensor_copy(gkrow[:, h, :], bank[3][:]).then_inc(g_krow, 1)
                    dve.drain()
                    with dve.Fori(0, NT) as it:
                        t = k * NT + it
                        nc.vector.tensor_copy(gqc[:], flat(gql)[:, bass.ds(it * H, H)])
                        dve.drain()
                        for h in range(H):
                            r = t * H + h
                            nc.vector.scalar_tensor_tensor(gt[:], gkrow[:, h, :], gqc[:, h:h + 1],
                                                           flat(gbias)[:, bass.ds(it * N, N)], ALU.add, ALU.add)
                            dve.drain()
                            nc.vector.scalar_tensor_tensor(gt2[:], gt[:], 0.01, gt[:], ALU.mult, ALU.max)
                            dve.drain()
                            head(dve, 1, r, go[:], bank[3][:, 0:D])
                            dve.drain()
                            nc.vector.tensor_copy(gst[:, 0:1], grec[:]).then_inc(g_o[1], 1)
                            dve.wait_ge(g_oT_ps[1], r + 1)
                            nc.vector.tensor_copy(goT[:], bank[5][:, 0:P]).then_inc(g_oT[1], 1)
                        dve.wait_ge(g_y_ps[1], t + 1)
                        nc.vector.tensor_tensor(gz[:], bank[4][:, 0:D], fpb[:], ALU.add)
                        dve.drain()
                        nc.vector.tensor_tensor(gz[:], gz[:], flat(gx1)[:, bass.ds(it * D, D)], ALU.add).then_inc(g_z, 1)
                        dve.wait_ge(g_sig, t + 1)
                        nc.vector.tensor_scalar(gz[:], gln[:], 0.5, 0.5, ALU.mult, ALU.add)
                        dve.drain()
                        nc.vector.tensor_tensor(flat(gx)[:, bass.ds(it * D, D)], gz[:],
                                                flat(gx1)[:, bass.ds(it * D, D)], ALU.add)
                        dve.drain()
                    layernorm(dve, gy, gx, 1, f).then_inc(g_y, 1)

        def head(dve, layer, r, dst, o_ps):
            nc.vector.tensor_reduce(gst[:, 0:1], gt2[:], AX_X, ALU.max)
            dve.drain()
            nc.vector.tensor_scalar(gmax[:], gst[:, 0:1], -1.0, None, ALU.mult).then_inc(g_max[layer], 1)
            dve.wait_ge(g_exp[layer], r + 1)
            nc.vector.reciprocal(grec[:], gsum[:])
            dve.wait_ge(g_pT_ps[layer], r + 1)
            nc.vector.tensor_copy(gpT[:].rearrange("p t n -> p (t n)"), bank[2][:]).then_inc(g_pT[layer], 1)
            dve.wait_ge(g_o_ps[layer], r + 1)
            nc.vector.tensor_scalar(dst, o_ps, grec[:, 0:1], None, ALU.mult)

        def general_tensor(pe):
            with pe.Fori(0, B) as b:
                needed, k = turn(pe, b)
                f = k + 1
                with pe.If(needed > 0):
                    pe.wait_ge(g_in, f * 32)
                    for t in range(NT):
                        last = nc.tensor.transpose(bank[0][:, t * P:(t + 1) * P], gx[:, t, :], ident[:])
                    last.then_inc(g_xT_ps, 1)
                    pe.wait_ge(g_xT, f)
                    for g in range(G):
                        mm(bank[1 + g][:], wqTg[:, g, :], gxT[:])
                        mm(bank[1 + G + g][:], wkTg[:, g, :], gxT[:])
                    for t in range(NT):
                        last = mm(bank[1 + 2 * G][:, t * P:(t + 1) * P], gxT[:, t * P:(t + 1) * P], wvT[:])
                    last.then_inc(g_proj_ps, 1)
                    with pe.Fori(0, NT) as it:
                        t = k * NT + it
                        pe.wait_ge(g_proj, f)
                        pe.wait_ge(g_tile, t + 1)
                        for h in range(H):
                            r = t * H + h
                            c = 32 * (h % HG)
                            mm(bank[0][:], gqt[c:c + 32, h // HG, :], gk[c:c + 32, h // HG, :]).then_inc(g_score[0], 1)
                            pe.wait_ge(g_exp[0], r + 1)
                            for j in range(NT):
                                last = nc.tensor.transpose(bank[2][:, j * P:(j + 1) * P], gp[:, j * P:(j + 1) * P], ident[:])
                            last.then_inc(g_pT_ps[0], 1)
                            pe.wait_ge(g_pT[0], r + 1)
                            for j in range(NT):
                                last = mm(bank[3][:, h * HD:(h + 1) * HD], gpT[:, j, :], gv[:, j, h * HD:(h + 1) * HD],
                                          j == 0, j == NT - 1)
                            last.then_inc(g_o_ps[0], 1)
                        pe.wait_ge(g_o[0], t + 1)
                        nc.tensor.transpose(bank[5][:, 0:P], go[:], ident[:]).then_inc(g_oT_ps[0], 1)
                        pe.wait_ge(g_oT[0], t + 1)
                        mm(bank[4][:, 0:D], goT[:], woT[:]).then_inc(g_y_ps[0], 1)
                    pe.wait_ge(g_x1, f)
                    for t in range(NT):
                        last = nc.tensor.transpose(bank[0][:, t * P:(t + 1) * P], gx1[:, t, :], ident[:])
                    last.then_inc(g_x1T_ps, 1)
                    pe.wait_ge(g_x1T, f)
                    for jt in range(NT):
                        if jt:
                            pe.wait_ge(g_fp, k * NT + jt)
                        for half in range(2):
                            cols = slice(half * 512, half * 512 + 512)
                            mm(bank[1 + half][:], gxT[:, jt * P:(jt + 1) * P], fcw[:, cols], True, False)
                            last = mm(bank[1 + half][:], ones[0:1, :], fcb[0:1, cols], False, True)
                        last.then_inc(g_fp_ps, 1)
                    for h in range(H):
                        pe.wait_ge(g_diag, k * H + h + 1)
                        if h:
                            pe.wait_ge(g_krow, k * H + h)
                        mm(bank[3][:], ones[:], gdiag[:].rearrange("p t n -> p (t n)")).then_inc(g_krow_ps, 1)
                    with pe.Fori(0, NT) as it:
                        t = k * NT + it
                        for h in range(H):
                            r = t * H + h
                            pe.wait_ge(g_exp[1], r + 1)
                            for j in range(NT):
                                last = nc.tensor.transpose(bank[2][:, j * P:(j + 1) * P], gp[:, j * P:(j + 1) * P], ident[:])
                            last.then_inc(g_pT_ps[1], 1)
                            pe.wait_ge(g_pT[1], r + 1)
                            for j in range(NT):
                                last = mm(bank[3][:, 0:D], gpT[:, j, :], gfp[:, j, h * D:(h + 1) * D], j == 0, j == NT - 1)
                            last.then_inc(g_o_ps[1], 1)
                            pe.wait_ge(g_o[1], r + 1)
                            nc.tensor.transpose(bank[5][:, 0:P], go[:], ident[:]).then_inc(g_oT_ps[1], 1)
                            pe.wait_ge(g_oT[1], r + 1)
                            last = mm(bank[4][:, 0:D], goT[:], fpw[:, h, :], h == 0, h == H - 1)
                        last.then_inc(g_y_ps[1], 1)
                    pe.wait_ge(g_out, f * 16)



        class Graph:

            def __init__(self, base, off=0, eng=None, products=None):
                self.base, self.off, self.eng = base, off, eng
                self.static = isinstance(base, int)
                self.products = {} if products is None else products

            def up(self, k):
                return Graph(self.base, self.off + k, self.eng, self.products)

            def at(self, per, i, unit=1):
                if self.static:
                    return ((self.base + self.off) * per + i + 1) * unit
                if per * unit not in self.products:
                    self.products[per * unit] = self.eng.snap(self.base * (per * unit))
                return self.products[per * unit] + (self.off * per + i + 1) * unit

            @property
            def index(self):
                return bass.ds(self.base + self.off, 1)

        def bodies(eng, body):
            body(Graph(0, -1), 1, True, False, False)
            body(Graph(0), 0, True, True, False)
            with eng.Fori(1, B - 2, 2) as n:
                odd = Graph(n, 0, eng)
                body(odd, 1, True, True, True)
                body(odd.up(1), 0, True, True, True)
            body(Graph(B - 1), 1, False, True, True)
            body(Graph(B), 0, False, False, True)

        USES = (
            ("xT", 0, p_act, 0, 8, 1), ("t2g1", 1, normed, 1, 2, -1), ("q", 0, p_dve, 0, 6, 1), ("k", 1, p_dve, 1, 6, 1),
            ("onT", 0, t_act, 1, 4, -1), ("v", 1, p_act, 3, 8, 1), ("wo", 0, t_y, 0, 1, -1), ("a0", 1, p_act, 4, 8, 1),
            ("a1", 0, p_act, 5, 8, 1), ("oh0", 1, m_act, 1, 3, 0), ("t2g0", 0, normed, 0, 2, 0), ("a2", 1, p_act, 6, 8, 1),
            ("oh1", 0, m_act, 2, 3, 0), ("gather", 1, t_act, 2, 4, -1), ("a3", 0, p_act, 7, 8, 1), ("fold", 1, t_z, 0, 1, -1))
        NAMES = [u[0] for u in USES]

        def exists(rel, n, has_next, has_before, main):
            return {1: has_next, 0: main, -1: has_before}[rel]

        def bank_free(pe, name, n, has_next, main, has_before):
            i = NAMES.index(name)
            flags_now = {1: has_next, 0: main, -1: has_before}
            for back in range(i - 2, -1, -2):
                _, _, s, ev, per, rel = USES[back]
                if flags_now[rel]:
                    pe.wait_ge(s, n.up(rel).at(per, ev))
                    return
            if n.static:
                m = n.base + n.off - 1
                flags_then = {1: -1 <= m < B - 1, 0: 0 <= m < B, -1: 1 <= m}
                if m < -1:
                    return
            else:
                flags_then = {1: True, 0: True, -1: False}
            for back in range(len(USES) - 1 - ((len(USES) - 1 - i) % 2), -1, -2):
                _, _, s, ev, per, rel = USES[back]
                if flags_then[rel]:
                    pe.wait_ge(s, n.up(rel - 1).at(per, ev))
                    return

        def rows(src, m):
            src = src[m.index] if not m.static else src[m.base + m.off:m.base + m.off + 1]
            return src.rearrange("o (t p) d -> p (o t) d", p=P)

        def mbank(name):
            return M_BANK[USES[NAMES.index(name)][1]]

        def mm(o, l, r, start=True, stop=True):
            return nc.tensor.matmul(o, l, r, start=start, stop=stop)

        def fast_tensor(pe, n, p, nxt, main, bef):
            def scores(m, s, par):
                g, jt, hp = s // (2 * NT), (s // 2) % NT, s % 2
                if s == 0:
                    pe.wait_ge(stack_in, m.at(12, 11, 16))
                for e in range(2):
                    c = 2 * hp + e
                    h = g * HG + c
                    if not (m.static and m.base + m.off == 0 and s < 2):
                        pe.wait_ge(biased, m.at(2 * HALF, 2 * (s - 2) + e))
                    mm(S_BANK[c][:], QK[par][0:KR, 1, h, jt * P:(jt + 1) * P], QK[par][0:KR, 0, h, :]).then_inc(qk_ready, 1)

            def values(m, quad, par):
                g, jt = quad // NT, quad % NT
                pe.wait_ge(exped, m.at(HALF, 2 * quad + 1))
                if jt == 0 and not (m.static and m.base + m.off == 0):
                    pe.wait_ge(*((m_act, m.up(-1).at(3, 0)) if g == 0 else (t_act, m.up(-1).at(4, 0))))
                for c in range(HG):
                    last = nc.tensor.matmul(O_BANK[g][32 * c:32 * c + 32, :], V[par][:, jt, g * HG + c, :],
                                            TE[(2 * quad + c // 2) % 4][:, c % 2, :], start=jt == 0, stop=jt == NT - 1,
                                            tile_position=(0, 32 * c))
                last.then_inc(pv_done, 1)

            def shared(name, when=True):
                if when:
                    bank_free(pe, name, n, nxt, main, bef)
                return when

            nx, pv = n.up(1), n.up(-1)
            for s in range(HALF):
                if main and s < HALF - 1:
                    scores(n, s + 1, p)
                if s == HALF - 1 and nxt:
                    scores(nx, 0, 1 - p)
                if bef and s == 1:
                    values(pv, 2 * NT - 1, 1 - p)
                if main and s >= 3 and s % 2:
                    values(n, (s - 3) // 2, p)
                if s == 2 and shared("xT", nxt):
                    pe.wait_ge(x_in, nx.at(1, 0, 16))
                    for t in range(NT):
                        last = nc.tensor.transpose(mbank("xT")[:, t * P:(t + 1) * P], X[:, t, :], ident[:])
                    last.then_inc(p_full, 1)
                if s == 3 and shared("t2g1", bef):
                    pe.wait_ge(t_act, pv.at(4, 0))
                    for t in range(NT):
                        last = nc.tensor.transpose(mbank("t2g1")[:, t * P:(t + 1) * P], OS[:, 1, t * P:(t + 1) * P], ident[:])
                    last.then_inc(t_full, 1)
                if s == 4 and nxt:
                    shared("q")
                    pe.wait_ge(p_act, nx.at(8, 0))
                    mm(mbank("q")[:], wqT[:], XT[:]).then_inc(p_full, 1)
                    shared("k")
                    mm(mbank("k")[:], wkT[:], XT[:]).then_inc(p_full, 1)
                if s == 5 and shared("onT", bef):
                    pe.wait_ge(normed, pv.at(2, 1))
                    for t in range(NT):
                        last = nc.tensor.transpose(mbank("onT")[:, t * P:(t + 1) * P],
                                                   ON[:, t, :, :].rearrange("p h d -> p (h d)"), ident[:])
                    last.then_inc(t_full, 1)
                if s == 6 and shared("v", nxt):
                    for t in range(NT):
                        last = mm(mbank("v")[:, t * P:(t + 1) * P], XT[:, t * P:(t + 1) * P], wvT[:])
                    last.then_inc(p_full, 1)
                if s == 7 and shared("wo", bef):
                    pe.wait_ge(t_act, pv.at(4, 1))
                    for t in range(NT):
                        last = mm(mbank("wo")[:, t * P:(t + 1) * P], ONT[:, t * P:(t + 1) * P], woT[:])
                    last.then_inc(t_full, 1)

                def adjT(j):
                    if shared(f"a{j}", nxt):
                        pe.wait_ge(a_in, nx.at(1, 0, 16))
                        for t in range(NT):
                            last = nc.tensor.transpose(mbank(f"a{j}")[:, t * P:(t + 1) * P],
                                                       A[1 - p][:, t, j * P:(j + 1) * P], ident[:])
                        last.then_inc(p_full, 1)

                def onehotT(k):
                    if shared(f"oh{k}", main):
                        pe.wait_ge(onehot, n.at(4, 3))
                        o = mbank(f"oh{k}")[:].bitcast(bf16)
                        for j in range(2):
                            for t in range(NT):
                                last = nc.tensor.transpose(o[:, j * N + t * P:j * N + (t + 1) * P],
                                                           OH[:, t, (2 * k + j) * P:(2 * k + j + 1) * P], identb[:])
                        last.then_inc(m_full, 1)

                if s == 8:
                    adjT(0)
                if s == 9:
                    adjT(1)
                if s == 10:
                    onehotT(0)
                if s == 11:
                    if shared("t2g0", main):
                        pe.wait_ge(m_act, n.at(3, 0))
                        for t in range(NT):
                            last = nc.tensor.transpose(mbank("t2g0")[:, t * P:(t + 1) * P], OS[:, 0, t * P:(t + 1) * P],
                                                       ident[:])
                        last.then_inc(m_full, 1)
                    adjT(2)
                if s == 12:
                    onehotT(1)
                    if shared("gather", bef):
                        pe.wait_ge(t_cs, pv.at(1, 0))
                        pe.wait_ge(m_act, pv.at(3, 2))
                        for k in range(3):
                            for j in range(NT):
                                last = mm(mbank("gather")[:], CS[:, k, j, :], PT[1 - p][:, j, :], k == 0 and j == 0,
                                          k == 2 and j == NT - 1)
                        last.then_inc(t_full, 1)
                if s == 13:
                    adjT(3)
                    if shared("fold", bef):
                        pe.wait_ge(t_act, pv.at(4, 2))
                        for t in range(NT):
                            last = mm(mbank("fold")[:, t * P:(t + 1) * P], GT[:, t * P:(t + 1) * P], wf[:])
                        last.then_inc(t_full, 1)

        def fast_scalar(act, n, p, nxt, main, bef):
            nx, pv = n.up(1), n.up(-1)

            def take(per, sem_, ev, m, out_, in_, done):
                act.wait_ge(sem_, m.at(per, ev))
                nc.scalar.copy(out_, in_).then_inc(done, 1)

            for s in range(HALF):
                if s == 13 and bef:
                    take(5, t_full, 3, pv, GT[:], mbank("gather")[:], t_act)
                if main:
                    act.wait_ge(biased, n.at(2 * HALF, 2 * s + 1))
                    nc.scalar.activation(TE[s % 4][:], TE[s % 4][:], ACT.Exp).then_inc(exped, 1)
                if s == 2 and bef:
                    take(8, pv_done, 7, pv, OS[:, 1, :], O_BANK[1][:], t_act)
                if s == 2 and nxt:
                    take(8, p_full, 0, nx, XT[:], mbank("xT")[:], p_act)
                if s == 4 and nxt:
                    if not (n.static and n.base + n.off == -1):
                        act.wait_ge(spl_out, n.at(1, 0, 16))
                    take(8, p_full, 1, nx, SPL[:, 0, 0, :], mbank("q")[:], p_act)
                    take(8, p_full, 2, nx, SPL[:, 1, 0, :], mbank("k")[:], p_act)
                if s == 6 and bef:
                    take(5, t_full, 1, pv, ONT[:], mbank("onT")[:], t_act)
                if s == 7 and nxt:
                    act.wait_ge(p_full, nx.at(8, 3))
                    act.wait_ge(s_vones, 1)
                    for t in range(NT):
                        last = nc.scalar.copy(V[1 - p][:, t, :, 0:HD],
                                              mbank("v")[:, t * P:(t + 1) * P].rearrange("p (h d) -> p h d", h=H))
                    last.then_inc(p_act, 1)
                if s == 10 and main:
                    take(8, pv_done, 3, n, OS[:, 0, :], O_BANK[0][:], m_act)
                for j, when in enumerate((8, 9, 11, 13)):
                    if s == when and nxt:
                        take(8, p_full, 4 + j, nx, AT[1 - p][:, 0, j, :], mbank(f"a{j}")[:], p_act)
                for k, when in enumerate((10, 12)):
                    if s == when and main:
                        act.wait_ge(m_full, n.at(3, 2 * k))
                        nc.scalar.copy(PT[p][:, 2 * k:2 * k + 2, :].rearrange("p t n -> p (t n)"),
                                       mbank(f"oh{k}")[:].bitcast(bf16)).then_inc(m_act, 1)
                if s == 14 and bef:
                    act.wait_ge(t_z, pv.at(1, 0))
                    nc.scalar.activation(TH[:], Z[:], ACT.Tanh, scale=0.5).then_inc(t_act, 1)

        def fast_vector(dve, n, p, nxt, main, bef):
            nx, pv = n.up(1), n.up(-1)

            def bias(s, e):
                g, jt, hp = s // (2 * NT), (s // 2) % NT, s % 2
                c = 2 * hp + e
                h = g * HG + c
                if s == 0 and e == 0:
                    dve.wait_ge(a_in, n.at(1, 0, 16))
                if e == 0:
                    if s % 2 == 0 and g == 0:
                        dve.wait_ge(p_pool, n.at(6, 2 + jt))
                    if not (n.static and n.base + n.off == 0 and s < 4):
                        dve.wait_ge(pv_done, n.at(8, (s - 4) // 2))
                dve.wait_ge(qk_ready, n.at(2 * HALF, 2 * s + e))
                flat = AT[p][:].rearrange("p a t n -> p (a t n)")
                nc.vector.scalar_tensor_tensor(TE[s % 4][:, e, :], flat[:, bass.ds(signs[h] + jt * N, N)],
                                               we[:, h:h + 1], S_BANK[c][:], ALU.mult, ALU.add).then_inc(biased, 1)

            def side(s, part):
                if main and s < NT and part == 0:
                    nc.vector.max(MX[p][:, s, :], A[p][:, s, :]).then_inc(maxed, 1)
                if main and s < NT and part == 1:
                    dve.wait_ge(maxed, n.at(4, s))
                    if s == 0 and not (n.static and n.base + n.off == 0):
                        dve.wait_ge(m_full, n.up(-1).at(3, 2))
                    nc.vector.tensor_scalar(OH[:, s, :], A[p][:, s, :], MX[p][:, s, 0:1], None, ALU.is_ge).then_inc(onehot, 1)

                def norm(g, m, full, ev, per, name, rd):
                    o = mbank(name)[:].rearrange("p (t h c) -> p t h c", t=NT, h=HG)
                    if part == 0:
                        dve.wait_ge(full, m.at(per, ev))
                        nc.vector.reciprocal(rd[:, g, :, :], o[:, :, :, HD]).then_inc(recip, 1)
                    else:
                        dve.wait_ge(recip, m.at(2, g))
                        for t in range(NT):
                            last = nc.vector.tensor_tensor(
                                ON[:, t, g * HG:(g + 1) * HG, :], o[:, t, :, 0:HD],
                                rd[:, g, t, :].rearrange("p (h o) -> p h o", o=1).to_broadcast([P, HG, HD]), ALU.mult)
                        last.then_inc(normed, 1)

                if s == 4 and bef:
                    norm(1, pv, t_full, 0, 5, "t2g1", RD[1 - p])
                if s == 12 and main:
                    norm(0, n, m_full, 1, 3, "t2g0", RD[p])
                if s == 5 and nxt:
                    dve.wait_ge(p_act, nx.at(8, 1 + part))
                    nc.vector.tensor_tensor(RES[:, part, :], mbank("qk"[part])[:], SPL[:, part, 0, :],
                                            ALU.subtract).then_inc(p_dve, 1)
                if bef and (s, part) == (8, 0):
                    dve.wait_ge(t_full, pv.at(5, 2))
                    dve.wait_ge(xr_in, pv.at(1, 0, 16))
                    nc.vector.tensor_tensor(Y[:].rearrange("p t d -> p (t d)"), mbank("wo")[:],
                                            XR[:].rearrange("p t d -> p (t d)"), ALU.add).then_inc(t_y, 1)
                if bef and (s, part) in ((8, 1), (15, 1)):
                    layer = int(s == 15)
                    src = (Y, U)[layer]
                    dve.wait_ge(*((t_y, pv.at(1, 0)) if layer == 0 else (t_u, pv.at(1, 0))))
                    for t in range(NT):
                        nc.vector.bn_stats(ST[:, t, :], src[:, t, :])
                if bef and ((s, part) == (9, 0) or (s, part) == (15, 1)):
                    layer = int(s == 15)
                    dve.drain()
                    for t in range(NT):
                        last = nc.vector.bn_aggr(MV[:, layer, t, :], ST[:, t, :])
                    last.then_inc(t_mv, 1)
                for j, when in enumerate(((9, 1), (10, 1), (12, 0), (14, 1))):
                    if nxt and (s, part) == when:
                        dve.wait_ge(p_act, nx.at(8, 4 + j))
                        nc.vector.tensor_scalar(MT[:, j, :], AT[1 - p][:, 0, j, :], 0.0, -BIG, ALU.is_equal,
                                                ALU.mult).then_inc(p_dve, 1)
                if bef and (s, part) == (14, 0):
                    dve.wait_ge(t_full, pv.at(5, 4))
                    dve.wait_ge(t_xb, pv.at(1, 0))
                    nc.vector.tensor_tensor(Z[:].rearrange("p t d -> p (t d)"), mbank("fold")[:],
                                            XB[:].rearrange("p t d -> p (t d)"), ALU.add).then_inc(t_z, 1)
                if bef and (s, part) == (15, 0):
                    dve.wait_ge(t_act, pv.at(4, 3))
                    nc.vector.scalar_tensor_tensor(U[:].rearrange("p t d -> p (t d)"), TH[:].rearrange("p t d -> p (t d)"), 0.5,
                                                   XH[:].rearrange("p t d -> p (t d)"), ALU.mult, ALU.add).then_inc(t_u, 1)

            for s in range(HALF):
                for part in range(2):
                    if main:
                        bias(s, part)
                    side(s, part)

        def fast_gpsimd(pool, n, p, nxt, main, bef):
            nx, pv = n.up(1), n.up(-1)
            G_ = nc.gpsimd

            def alone(m):
                if not m.static:
                    G_.tensor_tensor(CD[:, 0, 0:1], mhalf[:, 0:1], mhalf[:, 0:1], ALU.mult)

            flat = lambda m: m[:].rearrange("p t d -> p (t d)")
            if nxt:
                for a in range(2):
                    pool.wait_ge(p_dve, nx.at(6, a))
                    alone(n)
                    G_.tensor_scalar(SPL[:, a, 1, :], RES[:, a, :], 1.0, 0.0, ALU.mult, ALU.add)
                    pool.drain()
                    G_.tensor_tensor(SPL[:, a, 2, :], RES[:, a, :], SPL[:, a, 1, :], ALU.subtract).then_inc(p_pool, 1)

            def scale(layer, dst, src, done):
                pool.wait_ge(t_mv, pv.at(2, layer))
                alone(n)
                G_.tensor_scalar(VAR[:, layer, :], MV[:, layer, :, 1], 1.0, EPS, ALU.mult, ALU.add)
                G_.tensor_scalar(NM[:, layer, :], MV[:, layer, :, 0], -1.0, 0.0, ALU.mult, ALU.add)
                pool.drain()
                G_.tensor_tensor(RS[:, layer, :], VAR[:, layer, :], mhalf[:, 0:NT], ALU.pow)
                pool.drain()
                for t in range(NT):
                    last = G_.tensor_scalar(dst[:, t, :], src[:, t, :], NM[:, layer, t:t + 1], RS[:, layer, t:t + 1],
                                            ALU.add, ALU.mult)
                last.then_inc(done, 1)

            def masked(j):
                if nxt:
                    pool.wait_ge(p_dve, nx.at(6, 2 + j))
                    G_.tensor_tensor(AT[1 - p][:, 1, j, :], AT[1 - p][:, 0, j, :], MT[:, j, :], ALU.subtract)
                    pool.drain()
                    G_.tensor_tensor(AT[1 - p][:, 0, j, :], AT[1 - p][:, 0, j, :], MT[:, j, :], ALU.add).then_inc(p_pool, 1)

            if bef:
                q = 1 - p
                m2 = CK[:, 0, :].rearrange("p (t k) -> p t k", t=NT)
                b2 = CK[:, 1, :].rearrange("p (t k) -> p t k", t=NT)
                l2 = CK[:, 2, :].rearrange("p (t k) -> p t k", t=NT)
                w2 = CK[:, 3, :].rearrange("p (t k) -> p t k", t=NT)
                G_.tensor_scalar(m2, MX[q][:, :, 0:2], -1.0, 1.0, ALU.mult, ALU.add)
                pool.drain()
                G_.tensor_scalar(b2, m2, NEG, 0.0, ALU.mult, ALU.add)
                pool.drain()
                G_.tensor_scalar(w2, b2, 0.0, 0.0, ALU.max, ALU.add)
                G_.tensor_scalar(m2, b2, 0.0, 0.0, ALU.min, ALU.add)
                pool.drain()
                G_.tensor_scalar(l2, m2, 0.01, 0.0, ALU.mult, ALU.add)
                pool.wait_ge(recip, pv.at(2, 1))
                G_.tensor_tensor(b2, w2, m2, ALU.subtract)
                pool.drain()
                G_.tensor_tensor(l2, l2, w2, ALU.add)
                G_.tensor_tensor(b2[:, :, 0], b2[:, :, 0], b2[:, :, 1], ALU.add)
                pool.drain()
                G_.tensor_tensor(l2[:, :, 0], l2[:, :, 0], l2[:, :, 1], ALU.subtract)
                G_.tensor_scalar(b2[:, :, 0], b2[:, :, 0], 2.0 ** -21, gapmin[:, 0:1], ALU.mult, ALU.add)
                pool.drain()
                G_.tensor_tensor(l2[:, :, 0], l2[:, :, 0], b2[:, :, 0], ALU.subtract)
                pool.drain()
                G_.tensor_scalar(w2[:, :, 0], l2[:, :, 0], 0.0, None, ALU.is_ge)
                r = RD[q][:].rearrange("p g t h -> p (g t h)")
                G_.tensor_scalar(CD[:, 0, :], r, 1e20, None, ALU.is_le)
                G_.tensor_scalar(CD[:, 1, :], r, 1e-30, None, ALU.is_ge)
                pool.drain()
                G_.tensor_tensor(CD[:, 2, :], CD[:, 0, :], CD[:, 1, :], ALU.mult)
                pool.drain()
                for half_ in (16, 8, 4):
                    G_.tensor_tensor(CD[:, 2, 0:half_], CD[:, 2, 0:half_], CD[:, 2, half_:2 * half_], ALU.mult)
                    pool.drain()
                G_.tensor_tensor(w2[:, :, 0], w2[:, :, 0], CD[:, 2, 0:NT], ALU.mult)
                pool.drain()
                G_.tensor_tensor(w2[:, 0:2, 0], w2[:, 0:2, 0], w2[:, 2:4, 0], ALU.mult)
                pool.drain()
                bcol = checks[:, pv.base + pv.off:pv.base + pv.off + 1] if pv.static else checks[:, bass.ds(pv.base + pv.off, 1)]
                G_.tensor_tensor(bcol, w2[:, 0:1, 0], w2[:, 1:2, 0], ALU.mult).then_inc(t_ck, 1)
            if bef:
                scale(0, X1, Y, t_x1)
                pool.drain()
                G_.tensor_scalar(flat(CS[:, 0]), flat(X1), 1.0, 0.0, ALU.mult, ALU.add)
                pool.drain()
                G_.tensor_tensor(flat(CR), flat(X1), flat(CS[:, 0]), ALU.subtract)
                pool.drain()
                G_.tensor_scalar(flat(CS[:, 1]), flat(CR), 1.0, 0.0, ALU.mult, ALU.add)
                pool.drain()
                G_.tensor_tensor(flat(CS[:, 2]), flat(CR), flat(CS[:, 1]), ALU.subtract).then_inc(t_cs, 1)
                for t in range(NT):
                    G_.tensor_tensor(XB[:, t, :], X1[:, t, :], bf[:], ALU.add)
                G_.tensor_scalar(flat(XH), flat(X1), 1.0, 0.5, ALU.mult, ALU.add).then_inc(t_xb, 1)
            masked(0)
            masked(1)
            if bef:
                scale(1, OUT, U, t_out)
                pool.wait_ge(t_out, pv.at(1, 0))
                pool.dma_start(rows(out, pv), OUT[:]).then_inc(out_st, 16)
            masked(2)
            masked(3)
            if bef:
                pool.wait_ge(out_st, pv.at(1, 0, 16))
        def fast_sync(sp, n, p, nxt, main, bef):
            nx, pv = n.up(1), n.up(-1)
            first = n.static and n.base + n.off == -1
            second = n.static and n.base + n.off == 0
            at = lambda m, *a: m.at(*a) if m.static else sp.snap(m.at(*a))
            if nxt:
                x_free = at(n, 8, 0)
                parts_made, parts_out = at(nx, 6, 1), at(nx, 1, 0, 16)
                if not first and not second:
                    onehots, scored = at(n.up(-1), 4, 3), at(n, 2 * HALF, 0)
            if bef:
                y_made = at(pv, 1, 0)
            if nxt:
                if not first:
                    sp.wait_ge(p_full, x_free)
                sp.dma_start(X[:], rows(x, nx)).then_inc(x_in, 16)
                if not first and not second:
                    sp.wait_ge(onehot, onehots)
                sp.dma_start(A[1 - p][:], rows(adj, nx)).then_inc(a_in, 16)
            if bef:
                sp.dma_start(XR[:], rows(x, pv)).then_inc(xr_in, 16)
                sp.wait_ge(t_y, y_made)
            if nxt:
                sp.wait_ge(p_pool, parts_made)
                sp.dma_start(scratch[1 - p], SPL[:]).then_inc(spl_out, 16)
                sp.wait_ge(spl_out, parts_out)
                if not first and not second:
                    sp.wait_ge(qk_ready, scored)
                for r, parts in enumerate(PARTS):
                    for a in range(2):
                        sp.dma_start(QK[1 - p][HD * r:HD * r + HD, a, :, :],
                                     scratch[1 - p, :, a, parts[a], :].rearrange("(h d) i -> d h i", h=H)).then_inc(stack_in, 16)

        block = ctx.enter_context(nc.Block())

        @block.sync
        def _(sp):
            for dst, src in ((wq_rows, W_q), (wk_rows, W_k), (wv_rows, W_v), (wo_rows, W_o), (fcw[:], fc_w)):
                sp.dma_start(dst, src).then_inc(s_w, 16)
            sp.dma_start(we[:], W_e.rearrange("h o -> o h").to_broadcast([P, H])).then_inc(s_w, 16)
            sp.dma_start(fcb[:], fc_b.rearrange("(o n) -> o n", o=1)).then_inc(s_w, 16)
            sp.dma_start(fcb8[:], fc_b.rearrange("(h n) -> h n", h=H)).then_inc(s_w, 16)
            sp.dma_start(fpw[:], fp_w.rearrange("(h c) n -> c h n", h=H)).then_inc(s_w, 16)
            sp.dma_start(fpb[:], fp_b.rearrange("(o n) -> o n", o=1).to_broadcast([P, D])).then_inc(s_w, 16)
            sp.dma_start(qw[:], q_w.rearrange("n o -> o n").to_broadcast([P, D])).then_inc(s_w, 16)
            sp.dma_start(kw[:], k_w.rearrange("n o -> o n").to_broadcast([P, D])).then_inc(s_w, 16)
            sp.dma_start(qkcol[:, 0:1], q_w).then_inc(s_w, 16)
            sp.dma_start(qkcol[:, 1:2], k_w).then_inc(s_w, 16)
            sp.dma_start(qkb[:, 0:1], q_b.rearrange("(o n) -> o n", o=1).to_broadcast([P, 1])).then_inc(s_w, 16)
            sp.dma_start(qkb[:, 1:2], k_b.rearrange("(o n) -> o n", o=1).to_broadcast([P, 1])).then_inc(s_w, 16)
            bodies(sp, lambda *a: fast_sync(sp, *a))
            last = Graph(B - 1)
            sp.wait_ge(out_st, last.at(1, 0, 16))
            sp.wait_ge(s_flags, 1)
            general_sync(sp)

        @block.gpsimd
        def _(pool):
            pool.memset(ident[:], 0.0).then_inc(s_c, 1)
            pool.memset(tri[:], 0.0).then_inc(s_c, 1)
            pool.wait_ge(s_c, 2)
            pool.affine_select(out=ident[:], in_=ident[:], compare_op=ALU.not_equal, fill=1.0, base=0,
                               pattern=[[-1, P]], channel_multiplier=1).then_inc(s_c, 1)
            pool.affine_select(out=tri[:, 0:B], in_=tri[:, 0:B], compare_op=ALU.not_equal, fill=1.0, base=0,
                               pattern=[[-1, B]], channel_multiplier=1).then_inc(s_c, 1)
            pool.affine_select(out=tri[:, B:2 * B], in_=tri[:, B:2 * B], compare_op=ALU.is_ge, fill=1.0, base=0,
                               pattern=[[-1, B]], channel_multiplier=1).then_inc(s_c, 1)
            pool.memset(ones[:], 1.0).then_inc(s_c, 1)
            pool.memset(mhalf[:], -0.5).then_inc(s_c, 1)
            pool.memset(phalf[:], 0.5).then_inc(s_c, 1)
            for i in range(2):
                last = pool.memset(V[i][:], 1.0)
            last.then_inc(s_vones, 1)
            pool.wait_ge(s_norm, 1)
            nc.gpsimd.tensor_tensor(nrm[:, 0:2 * H], nsq[:, 0:2 * H], phalf[:], ALU.pow).then_inc(s_root, 1)
            pool.wait_ge(s_const, 1)
            bodies(pool, lambda *a: fast_gpsimd(pool, *a))
            pool.wait_ge(s_flags, 1)
            general_gpsimd(pool)

        @block.scalar
        def _(act):
            act.wait_ge(s_const, 1)
            bodies(act, lambda *a: fast_scalar(act, *a))
            act.wait_ge(s_flags, 1)
            general_scalar(act)

        @block.vector
        def _(dve):
            dve.wait_ge(s_wT_ps, 1)
            nc.vector.tensor_scalar(wqT[:], bank[0][:, 0:P], float(HD) ** -0.5, None, ALU.mult)
            nc.vector.tensor_copy(wkT[:], bank[0][:, P:2 * P])
            nc.vector.tensor_copy(wvT[:], bank[0][:, 2 * P:3 * P])
            nc.vector.tensor_copy(woT[:], bank[0][:, 3 * P:4 * P])
            nc.vector.memset(wqTg[:], 0.0)
            nc.vector.memset(wkTg[:], 0.0)
            nc.vector.tensor_copy(identb[:], ident[:])
            nc.vector.tensor_copy(fcT[:, 0:4, :], bank[1][:].rearrange("p (h d) -> p h d", h=4))
            nc.vector.tensor_copy(fcT[:, 4:8, :], bank[2][:].rearrange("p (h d) -> p h d", h=4))
            nc.vector.tensor_copy(fcbT[:], bank[3][:, 0:H])
            dve.drain()
            for pad, w in ((wqTg, wqT), (wkTg, wkT)):
                nc.vector.tensor_copy(pad[:].rearrange("p g (c d) -> p (g c) d", d=32)[:, :, 0:HD],
                                      w[:].rearrange("p (h d) -> p h d", h=H))
            for h in range(H):
                nc.vector.tensor_scalar(fcB[:, h, :], ones[:], fcbT[:, h:h + 1], None, ALU.mult)
            for a, w in enumerate((qw, kw)):
                for h in range(H):
                    nc.vector.tensor_tensor(prod[:, h, :], fcw[:, h * D:(h + 1) * D], w[:], ALU.mult)
                dve.drain()
                nc.vector.tensor_reduce(nrm[:, a * H:(a + 1) * H], prod[:], AX_X, ALU.add)
                dve.drain()
                nc.vector.tensor_tensor(nsq[:, a * H:(a + 1) * H], nrm[:, a * H:(a + 1) * H], nrm[:, a * H:(a + 1) * H],
                                        ALU.mult)
                nc.vector.tensor_scalar(nsq[:, 2 * H + a * H:2 * H + (a + 1) * H], fcbT[:], qkcol[:, a:a + 1], None, ALU.mult)
            dve.drain()
            nc.vector.tensor_copy(gst[:, 0:1], ones[:, 0:1]).then_inc(s_fold_in, 1)
            dve.wait_ge(s_fold_ps, 1)
            nc.vector.tensor_copy(wf[:], bank[4][:, 0:D])
            nc.vector.tensor_tensor(bf[:], bank[5][:, 0:D], fpb[:], ALU.add)
            nc.vector.tensor_copy(nsq[:], bank[6][:, 0:4 * H])
            dve.drain()
            nc.vector.tensor_copy(gst[:, 0:1], ones[:, 0:1]).then_inc(s_norm, 1)
            for a in range(2):
                nc.vector.tensor_scalar(nsq[:, 2 * H + a * H:2 * H + (a + 1) * H], nsq[:, 2 * H + a * H:2 * H + (a + 1) * H],
                                        qkb[:, a:a + 1], None, ALU.add)
            dve.drain()
            nc.vector.tensor_scalar(nab[:], nsq[:, 2 * H:4 * H], -1.0, None, ALU.mult)
            dve.drain()
            nc.vector.tensor_tensor(nab[:], nab[:], nsq[:, 2 * H:4 * H], ALU.max)
            dve.drain()
            dve.wait_ge(s_root, 1)
            nc.vector.scalar_tensor_tensor(nab[:], nrm[:], 1.02 * float(D) ** 0.5, nab[:], ALU.mult, ALU.add)
            dve.drain()
            nc.vector.tensor_reduce(gst[:, 0:2], nab[:].rearrange("p (a h) -> p a h", a=2), AX_X, ALU.max)
            dve.drain()
            nc.vector.tensor_tensor(gst[:, 2:3], gst[:, 0:1], gst[:, 1:2], ALU.add)
            dve.drain()
            nc.vector.tensor_scalar(gapmin[:], gst[:, 2:3], 2.04, 112.0, ALU.mult, ALU.add)
            nc.vector.tensor_scalar(sgn[0:1, 0:H], we[0:1, :], 0.0, float(NT * N), ALU.is_lt, ALU.mult)
            nc.vector.tensor_tensor(wesq[:], we[:], we[:], ALU.mult)
            dve.drain()
            nc.vector.tensor_reduce(gst[:, 3:4], wesq[:], AX_X, ALU.min)
            dve.drain()
            nc.vector.tensor_scalar(weok[:], gst[:, 3:4], 1e-20, None, ALU.is_ge)
            nc.vector.tensor_copy(gst[:, 0:1], ones[:, 0:1]).then_inc(s_const, 1)
            dve.drain()
            for h in range(H):
                signs.append(dve.value_load(sgn[0:1, h:h + 1], min_val=0, max_val=NT * N))
            bodies(dve, lambda *a: fast_vector(dve, *a))
            dve.wait_ge(t_ck, Graph(B - 1).at(1, 0))
            nc.vector.tensor_scalar(checks[:], checks[:], weok[:, 0:1], None, ALU.mult)
            dve.drain()
            nc.vector.tensor_scalar(checks[:], checks[:], -1.0, 1.0, ALU.mult, ALU.add).then_inc(s_bad, 1)
            dve.wait_ge(s_cnt_ps, 1)
            nc.vector.tensor_scalar(fcol[:], bank[0][0:B, 0:1], 0.5, None, ALU.is_ge).then_inc(s_cnt, 1)
            dve.wait_ge(s_ord_ps, 1)
            nc.vector.tensor_copy(flags[:], bank[1][0:1, 0:2 * B]).then_inc(s_flags, 1)
            dve.wait_ge(s_flags, 1)
            general_vector(dve)

        @block.tensor
        def _(pe):
            pe.wait_ge(s_c, 8)
            pe.wait_ge(s_w, 16 * WEIGHT_LOADS)
            for i, w in enumerate((wq_rows, wk_rows, wv_rows, wo_rows)):
                nc.tensor.transpose(bank[0][:, i * P:(i + 1) * P], w, ident[:])
            for h in range(H):
                nc.tensor.transpose(bank[1 + h // 4][:, (h % 4) * P:(h % 4 + 1) * P], fcw[:, h * D:(h + 1) * D], ident[:])
            nc.tensor.transpose(bank[3][:, 0:H], fcb8[:], ident[0:H, 0:H]).then_inc(s_wT_ps, 1)
            pe.wait_ge(s_fold_in, 1)
            for h in range(H):
                mm(bank[4][:, 0:D], fcT[:, h, :], fpw[:, h, :], h == 0, h == H - 1)
            for h in range(H):
                mm(bank[5][:, 0:D], fcB[:, h, :], fpw[:, h, :], h == 0, h == H - 1)
            mm(bank[6][:, 0:4 * H], ones[:], nsq[:]).then_inc(s_fold_ps, 1)
            pe.wait_ge(s_const, 1)
            bodies(pe, lambda *a: fast_tensor(pe, *a))
            pe.wait_ge(s_bad, 1)
            mm(bank[0][0:B, 0:1], checks[:], ones[:, 0:1]).then_inc(s_cnt_ps, 1)
            pe.wait_ge(s_cnt, 1)
            mm(bank[1][0:1, 0:2 * B], fcol[:], tri[:]).then_inc(s_ord_ps, 1)
            pe.wait_ge(s_flags, 1)
            general_tensor(pe)


_INS = ['x', 'adj', 'L0_gnn_W_q', 'L0_gnn_W_k', 'L0_gnn_W_v', 'L0_gnn_W_e', 'L0_gnn_W_o', 'L1_gnn_fc_w', 'L1_gnn_fc_b',
        'L1_gnn_q_w', 'L1_gnn_q_b', 'L1_gnn_k_w', 'L1_gnn_k_b', 'L1_gnn_fp_w', 'L1_gnn_fp_b']


def kernel(**inputs):
    import numpy as _np
    import concourse.bacc as _bacc
    from concourse import mybir as _mybir
    from concourse.bass_utils import run_bass_kernel_spmd as _run

    nc = _bacc.Bacc("TRN2", target_bir_lowering=False, num_devices=1)
    arrays, args = {}, []
    for name in _INS:
        a = _np.ascontiguousarray(inputs[name])
        arrays[f"in_{name}_dram"] = a
        args.append(nc.dram_tensor(f"in_{name}_dram", a.shape, _mybir.dt.from_np(a.dtype), kind="ExternalInput").ap())
    o = nc.dram_tensor("out_0_dram", inputs["x"].shape, _mybir.dt.float32, kind="ExternalOutput").ap()
    gnn_kernel(nc, *args, o)
    r = _run(nc, [arrays], core_ids=[0])
    return r.results[0]["out_0_dram"]
```

```python
import concourse.bass as bass
from concourse import mybir
from contextlib import ExitStack


def gnn_kernel(nc, x, adj, W_q, W_k, W_v, W_e, W_o, fc_w, fc_b, q_w, q_b, k_w, k_b, fp_w, fp_b, out):
    fp32 = mybir.dt.float32
    bf16 = mybir.dt.bfloat16
    i32 = mybir.dt.int32
    ALU = mybir.AluOpType
    ACT = mybir.ActivationFunctionType
    AX_X = mybir.AxisListType.X

    B, N, D = x.shape
    H = W_e.shape[0]
    HD = D // H
    P = 128
    NT = N // P
    HG = P // 32
    G = H // HG
    NEG = -1000000000.0
    MASKED = -3.0e38
    BIG = 1.0e30
    EPS = 1e-5

    ctx = ExitStack()
    with ctx:
        def sb(name, shape, dt=fp32):
            return ctx.enter_context(nc.sbuf_tensor(name, shape, dt))

        def sem(name):
            return ctx.enter_context(nc.semaphore(name))

        STEPS = 2 * H
        RING = 2 * HG
        PARTS = ((0, 0), (0, 1), (1, 0), (1, 1), (0, 2), (2, 0))
        KR = HD * len(PARTS)

        ident = sb("ident", [P, P])
        identb = sb("identb", [P, P], bf16)
        ones = sb("ones", [P, P])
        tri = sb("tri", [B, 2 * B + 1])
        mhalf = sb("mhalf", [P, 2 * H])
        phalf = sb("phalf", [P, 2 * H])
        wqT = sb("wqT", [P, P])
        wkT = sb("wkT", [P, P])
        wvT = sb("wvT", [P, P])
        woT = sb("woT", [P, P])
        wqTg = sb("wqTg", [P, G, P])
        wkTg = sb("wkTg", [P, G, P])
        we = sb("we", [P, H])
        fcw = sb("fcw", [P, H * D])
        fpw = sb("fpw", [P, H, D])
        fpb = sb("fpb", [P, D])
        wf = sb("wf", [P, D])
        bf = sb("bf", [P, D])
        qw = sb("qw", [P, D])
        kw = sb("kw", [P, D])
        qkcol = sb("qkcol", [P, 2])
        qkb = sb("qkb", [P, 2])
        sgn = sb("sgn", [1, 2 * H], i32)
        gapmin = sb("gapmin", [P, 1])
        wesq = sb("wesq", [P, H])
        fine = sb("fine", [P, B])
        checks = sb("checks", [P, B])
        denoms = sb("denoms", [P, B, G * NT * HG])
        tops = sb("tops", [P, B, NT, 2])
        flags = sb("flags", [1, 2 * B + 1], i32)
        fcol = sb("fcol", [B, 1])
        weok = sb("weok", [P, 1])
        warm = sb("warm", [P, 1])
        nsq = sb("nsq", [P, 4 * H])
        nrm = sb("nrm", [P, 2 * H])
        nab = sb("nab", [P, 2 * H])
        fcb8 = sb("fcb8", [H, D])
        fcbT = sb("fcbT", [P, H])
        order = flags[0:1, B:2 * B]

        X = sb("X", [P, NT, D])
        XR = sb("XR", [P, NT, D])
        A = [sb(f"A{i}", [P, NT, N]) for i in range(2)]
        AT = [sb(f"AT{i}", [P, 2, NT, N]) for i in range(2)]
        MT = sb("MT", [P, NT, N])
        QK = [sb(f"QK{i}", [P, 2, H, N], bf16) for i in range(2)]
        SPL = sb("SPL", [P, 2, 3, N], bf16)
        RES = sb("RES", [P, 2, N])
        V = [sb(f"V{i}", [P, NT, H, 32]) for i in range(2)]
        TE = [sb(f"TE{i}", [P, 2, N]) for i in range(RING)]
        XT = sb("XT", [P, N])
        MX = [sb(f"MX{i}", [P, NT, 8]) for i in range(2)]
        OH = sb("OH", [P, NT, N], bf16)
        PT = [sb(f"PT{i}", [P, NT, N], bf16) for i in range(2)]
        OS = sb("OS", [P, G, N])
        RD = [sb(f"RD{i}", [P, G, NT, HG]) for i in range(2)]
        ON = sb("ON", [P, NT, H, HD])
        ONT = sb("ONT", [P, N])
        Y = sb("Y", [P, NT, D])
        ST = sb("ST", [P, 2, NT, 6])
        MV = sb("MV", [P, 2, NT, 2])
        VAR = sb("VAR", [P, 2, NT])
        RS = sb("RS", [P, 2, NT])
        NM = sb("NM", [P, 2, NT])
        X1 = sb("X1", [P, NT, D])
        CS = sb("CS", [P, 3, NT, D], bf16)
        CR = sb("CR", [P, NT, D])
        XB = sb("XB", [P, NT, D])
        XH = sb("XH", [P, NT, D])
        GT = sb("GT", [P, N])
        TH = sb("TH", [P, NT, D])
        U = TH
        OUT = sb("OUT", [P, NT, D])
        CD = sb("CD", [P, 1])
        CK = [A[0][:, t, 0:B * NT * 2].rearrange("p (b t k) -> p b t k", t=NT, k=2) for t in range(4)]
        CR2 = A[1][:, 0, :].rearrange("p (b r) -> p b r", b=B)

        wq_rows, wk_rows, wv_rows, wo_rows = (A[1][:, 0, i * P:(i + 1) * P] for i in range(4))
        fcqk = sb("fcqk", [P, 2 * H])
        fcT = A[1][:, 1:3, :].rearrange("p t n -> p (t n)").rearrange("p (h d) -> p h d", h=H)
        fcB = AT[1][:, 0, 0:2, :].rearrange("p t n -> p (t n)").rearrange("p (h d) -> p h d", h=H)

        gx = X
        gadj = A[0]
        gbias = A[1]
        gxT = XT
        qkf = QK[0][:].rearrange("p a h n -> p (a h n)").bitcast(fp32)
        fcb = QK[1][:].rearrange("p a h n -> p (a h n)").bitcast(fp32)[0:1, 0:H * D]
        gq = qkf[:, 0:G * N].rearrange("p (g n) -> p g n", g=G)
        gk = qkf[:, G * N:2 * G * N].rearrange("p (g n) -> p g n", g=G)
        gqt = qkf[:, 2 * G * N:2 * G * N + G * P].rearrange("p (g n) -> p g n", g=G)
        gv = Y
        gt = TE[0][:, 0, :]
        gt2 = TE[0][:, 1, :]
        gmax = sb("gmax", [P, 1])
        gp = TE[1][:, 0, :]
        gsum = sb("gsum", [P, 1])
        grec = sb("grec", [P, 1])
        gpT = CR
        go = sb("go", [P, D])
        goT = sb("goT", [P, P])
        gx1 = X1
        gy = OUT
        gfp = AT[0][:].rearrange("p a t n -> p (a t n)").rearrange("p (t n) -> p t n", t=NT)
        gkrow = AT[1][:].rearrange("p a t n -> p (a t) n")
        gprod = TE[2][:].rearrange("p a n -> p (a n)").rearrange("p (h d) -> p h d", h=H)
        gql = sb("gql", [P, NT, H])
        gkl = sb("gkl", [P, NT, H])
        gqc = sb("gqc", [P, H])
        gdiag = U
        gln = sb("gln", [P, D])
        gst = sb("gst", [P, 8])
        gstat = ST[:, 0]
        gmv = sb("gmv", [P, NT, 2])
        gvar = sb("gvar", [P, NT])
        grstd = sb("grstd", [P, NT])
        gz = sb("gz", [P, D])

        scratch = nc.dram_tensor("qk_parts", (2, P, 2, 3, N), bf16, kind="Internal").ap()

        S_PS = [ctx.enter_context(nc.psum_tensor(f"scores{i}", [P, 2, N], fp32)) for i in range(2)]
        O_BANK = ctx.enter_context(nc.psum_tensor("outputs", [P, N], fp32))
        M_BANK = [ctx.enter_context(nc.psum_tensor(f"shared{i}", [P, N], fp32)) for i in range(3)]
        bank = [S_PS[i // 2][:, i % 2, :] for i in range(4)] + [O_BANK[:]] + [m[:] for m in M_BANK]

        s_w = sem("s_w")
        s_c = sem("s_c")
        s_w2 = sem("s_w2")
        s_wT_ps = sem("s_wT_ps")
        s_fcT_ps = sem("s_fcT_ps")
        s_fcT = sem("s_fcT")
        s_fold_ps = sem("s_fold_ps")
        s_fold_in = sem("s_fold_in")
        s_const = sem("s_const")
        s_norm_ps = sem("s_norm_ps")
        s_norm = sem("s_norm")
        s_root = sem("s_root")
        s_vones = sem("s_vones")
        s_bad = sem("s_bad")
        s_cnt_ps = sem("s_cnt_ps")
        s_cnt = sem("s_cnt")
        s_ord_ps = sem("s_ord_ps")
        s_flags = sem("s_flags")

        x_in = sem("x_in")
        a_in = sem("a_in")
        xr_in = sem("xr_in")
        spl_out = sem("spl_out")
        stack_in = sem("stack_in")
        out_st = sem("out_st")
        p_full = sem("p_full")
        p_act = sem("p_act")
        p_dve = sem("p_dve")
        p_pool = sem("p_pool")
        qk_ready = sem("qk_ready")
        biased = sem("biased")
        exped = sem("exped")
        pv_done = sem("pv_done")
        onehot = sem("onehot")
        maxed = sem("maxed")
        m_full = sem("m_full")
        m_act = sem("m_act")
        recip = sem("recip")
        normed = sem("normed")
        t_full = sem("t_full")
        t_act = sem("t_act")
        t_th = sem("t_th")
        t_y = sem("t_y")
        t_u = sem("t_u")
        t_mv = sem("t_mv")
        t_rs = sem("t_rs")
        t_x1 = sem("t_x1")
        t_cs = sem("t_cs")
        t_xb = sem("t_xb")
        t_xh = sem("t_xh")
        t_out = sem("t_out")

        g_in = sem("g_in")
        g_xT_ps = sem("g_xT_ps")
        g_xT = sem("g_xT")
        g_proj_ps = sem("g_proj_ps")
        g_proj = sem("g_proj")
        g_tile = sem("g_tile")
        g_score = [sem("g_score0")]
        g_max = [sem("g_max0"), sem("g_max1")]
        g_exp = [sem("g_exp0"), sem("g_exp1")]
        g_pT_ps = [sem("g_pT_ps0"), sem("g_pT_ps1")]
        g_pT = [sem("g_pT0"), sem("g_pT1")]
        g_o_ps = [sem("g_o_ps0"), sem("g_o_ps1")]
        g_o = [sem("g_o0"), sem("g_o1")]
        g_oT_ps = [sem("g_oT_ps0"), sem("g_oT_ps1")]
        g_oT = [sem("g_oT0"), sem("g_oT1")]
        g_y_ps = [sem("g_y_ps0"), sem("g_y_ps1")]
        g_x1 = sem("g_x1")
        g_x1T_ps = sem("g_x1T_ps")
        g_x1T = sem("g_x1T")
        g_fp_ps = sem("g_fp_ps")
        g_fp = sem("g_fp")
        g_diag = sem("g_diag")
        g_krow_ps = sem("g_krow_ps")
        g_krow = sem("g_krow")
        g_z = sem("g_z")
        g_sig = sem("g_sig")
        g_y = sem("g_y")
        g_var = [sem("g_var0"), sem("g_var1")]
        g_rstd = [sem("g_rstd0"), sem("g_rstd1")]
        g_out = sem("g_out")

        WEIGHT_LOADS, OTHER_LOADS = 5, 10
        nc.disable_value_cache = True
        signs = []

        def turn(eng, b):
            needed = eng.value_load(flags[0:1, bass.ds(b, 1)], min_val=0, max_val=1)
            before = eng.value_load(order[0:1, bass.ds(b, 1)], min_val=0, max_val=B - 1)
            return needed, before

        def general_sync(sp):
            with sp.Fori(0, B) as b:
                needed, k = turn(sp, b)
                f = k + 1
                with sp.If(needed > 0):
                    sp.dma_start(gx[:], x[bass.ds(b, 1)].rearrange("o (t p) d -> p (o t) d", p=P)).then_inc(g_in, 16)
                    sp.dma_start(gadj[:], adj[bass.ds(b, 1)].rearrange("o (t p) n -> p (o t) n", p=P)).then_inc(g_in, 16)
                    sp.dma_start(fcb[:], fc_b.rearrange("(o n) -> o n", o=1)).then_inc(g_in, 16)
                    sp.wait_ge(g_y, f)
                    sp.dma_start(out[bass.ds(b, 1)].rearrange("o (t p) d -> p (o t) d", p=P), gy[:]).then_inc(g_out, 16)

        def general_scalar(act):
            with act.Fori(0, B) as b:
                needed, k = turn(act, b)
                f = k + 1
                with act.If(needed > 0):
                    for layer in (0, 1):
                        with act.Fori(0, NT) as it:
                            t = k * NT + it
                            for h in range(H):
                                r = t * H + h
                                act.wait_ge(g_max[layer], r + 1)
                                nc.scalar.activation(gp[:], gt2[:], ACT.Exp, bias=gmax[:, 0:1],
                                                     accum_out=gsum[:, 0:1]).then_inc(g_exp[layer], 1)
                            if layer:
                                act.wait_ge(g_z, t + 1)
                                nc.scalar.activation(gln[:], gz[:], ACT.Tanh, scale=0.5).then_inc(g_sig, 1)

        def layernorm(dve, dst, src, layer, f):
            for t in range(NT):
                nc.vector.bn_stats(gstat[:, t, :], src[:, t, :])
            dve.drain()
            for t in range(NT):
                nc.vector.bn_aggr(gmv[:, t, :], gstat[:, t, :])
            dve.drain()
            nc.vector.tensor_scalar(gvar[:], gmv[:, :, 1], EPS, None, ALU.add).then_inc(g_var[layer], 1)
            dve.wait_ge(g_rstd[layer], f)
            for t in range(NT):
                last = nc.vector.tensor_scalar(dst[:, t, :], src[:, t, :], gmv[:, t, 0:1], grstd[:, t:t + 1],
                                               ALU.subtract, ALU.mult)
            return last

        def general_gpsimd(pool):
            with pool.Fori(0, B) as b:
                needed, k = turn(pool, b)
                f = k + 1
                with pool.If(needed > 0):
                    for layer in (0, 1):
                        pool.wait_ge(g_var[layer], f)
                        nc.gpsimd.tensor_tensor(grstd[:], gvar[:], mhalf[:, 0:NT], ALU.pow).then_inc(g_rstd[layer], 1)

        def general_vector(dve):
            flat = lambda m: m[:].rearrange("p t n -> p (t n)")
            with dve.Fori(0, B) as b:
                needed, k = turn(dve, b)
                f = k + 1
                with dve.If(needed > 0):
                    dve.wait_ge(g_in, f * 48)
                    nc.vector.tensor_scalar(flat(gbias), flat(gadj), 0.0, MASKED, ALU.is_equal, ALU.mult)
                    dve.wait_ge(g_xT_ps, f)
                    nc.vector.tensor_copy(gxT[:], bank[0][:]).then_inc(g_xT, 1)
                    dve.wait_ge(g_proj_ps, f)
                    for g in range(G):
                        nc.vector.tensor_copy(gq[:, g, :], bank[1 + g][:])
                        nc.vector.tensor_copy(gk[:, g, :], bank[1 + G + g][:])
                    nc.vector.tensor_copy(flat(gv), bank[1 + 2 * G][:]).then_inc(g_proj, 1)
                    dve.drain()
                    with dve.Fori(0, NT) as it:
                        t = k * NT + it
                        for g in range(G):
                            last = nc.vector.tensor_copy(gqt[:, g, :], gq[:, g, bass.ds(it * P, P)])
                        last.then_inc(g_tile, 1)
                        for h in range(H):
                            r = t * H + h
                            dve.wait_ge(g_score[0], r + 1)
                            nc.vector.scalar_tensor_tensor(gt[:], flat(gadj)[:, bass.ds(it * N, N)], we[:, h:h + 1],
                                                           bank[0][:], ALU.mult, ALU.add)
                            dve.drain()
                            nc.vector.tensor_tensor(gt2[:], gt[:], flat(gbias)[:, bass.ds(it * N, N)], ALU.add)
                            dve.drain()
                            head(dve, 0, r, go[:, h * HD:(h + 1) * HD], bank[3][:, h * HD:(h + 1) * HD])
                        dve.drain()
                        nc.vector.tensor_copy(gst[:, 0:1], grec[:]).then_inc(g_o[0], 1)
                        dve.wait_ge(g_oT_ps[0], t + 1)
                        nc.vector.tensor_copy(goT[:], bank[5][:, 0:P]).then_inc(g_oT[0], 1)
                        dve.wait_ge(g_y_ps[0], t + 1)
                        nc.vector.tensor_tensor(flat(gy)[:, bass.ds(it * D, D)], bank[4][:, 0:D],
                                                flat(gx)[:, bass.ds(it * D, D)], ALU.add)
                    dve.drain()
                    layernorm(dve, gx1, gy, 0, f).then_inc(g_x1, 1)
                    nc.vector.tensor_scalar(flat(gbias), flat(gadj), -1.0, 1.0, ALU.mult, ALU.add)
                    dve.drain()
                    nc.vector.tensor_scalar(flat(gbias), flat(gbias), NEG, None, ALU.mult)
                    dve.wait_ge(g_x1T_ps, f)
                    nc.vector.tensor_copy(gxT[:], bank[0][:]).then_inc(g_x1T, 1)
                    for jt in range(NT):
                        dve.wait_ge(g_fp_ps, k * NT + jt + 1)
                        nc.vector.tensor_copy(gfp[:, jt, 0:512], bank[1][:])
                        nc.vector.tensor_copy(gfp[:, jt, 512:1024], bank[2][:]).then_inc(g_fp, 1)
                        dve.drain()
                        fp3 = gfp[:, jt, :].rearrange("p (h d) -> p h d", h=H)
                        for w, dst, n in ((qw, gql, 0), (kw, gkl, 1)):
                            for h in range(H):
                                nc.vector.tensor_tensor(gprod[:, h, :], fp3[:, h, :], w[:], ALU.mult)
                            dve.drain()
                            nc.vector.tensor_reduce(dst[:, jt, :], gprod[:], AX_X, ALU.add)
                            dve.drain()
                            nc.vector.tensor_scalar(dst[:, jt, :], dst[:, jt, :], qkb[:, n:n + 1], None, ALU.add)
                    dve.drain()
                    for h in range(H):
                        for jt in range(NT):
                            last = nc.vector.tensor_scalar(gdiag[:, jt, :], ident[:], gkl[:, jt, h:h + 1], None, ALU.mult)
                        last.then_inc(g_diag, 1)
                        dve.wait_ge(g_krow_ps, k * H + h + 1)
                        nc.vector.tensor_copy(gkrow[:, h, :], bank[3][:]).then_inc(g_krow, 1)
                    dve.drain()
                    with dve.Fori(0, NT) as it:
                        t = k * NT + it
                        nc.vector.tensor_copy(gqc[:], flat(gql)[:, bass.ds(it * H, H)])
                        dve.drain()
                        for h in range(H):
                            r = t * H + h
                            nc.vector.scalar_tensor_tensor(gt[:], gkrow[:, h, :], gqc[:, h:h + 1],
                                                           flat(gbias)[:, bass.ds(it * N, N)], ALU.add, ALU.add)
                            dve.drain()
                            nc.vector.scalar_tensor_tensor(gt2[:], gt[:], 0.01, gt[:], ALU.mult, ALU.max)
                            dve.drain()
                            head(dve, 1, r, go[:], bank[3][:, 0:D])
                            dve.drain()
                            nc.vector.tensor_copy(gst[:, 0:1], grec[:]).then_inc(g_o[1], 1)
                            dve.wait_ge(g_oT_ps[1], r + 1)
                            nc.vector.tensor_copy(goT[:], bank[5][:, 0:P]).then_inc(g_oT[1], 1)
                        dve.wait_ge(g_y_ps[1], t + 1)
                        nc.vector.tensor_tensor(gz[:], bank[4][:, 0:D], fpb[:], ALU.add)
                        dve.drain()
                        nc.vector.tensor_tensor(gz[:], gz[:], flat(gx1)[:, bass.ds(it * D, D)], ALU.add).then_inc(g_z, 1)
                        dve.wait_ge(g_sig, t + 1)
                        nc.vector.tensor_scalar(gz[:], gln[:], 0.5, 0.5, ALU.mult, ALU.add)
                        dve.drain()
                        nc.vector.tensor_tensor(flat(gx)[:, bass.ds(it * D, D)], gz[:],
                                                flat(gx1)[:, bass.ds(it * D, D)], ALU.add)
                        dve.drain()
                    layernorm(dve, gy, gx, 1, f).then_inc(g_y, 1)

        def head(dve, layer, r, dst, o_ps):
            nc.vector.tensor_reduce(gst[:, 0:1], gt2[:], AX_X, ALU.max)
            dve.drain()
            nc.vector.tensor_scalar(gmax[:], gst[:, 0:1], -1.0, None, ALU.mult).then_inc(g_max[layer], 1)
            dve.wait_ge(g_exp[layer], r + 1)
            nc.vector.reciprocal(grec[:], gsum[:])
            dve.wait_ge(g_pT_ps[layer], r + 1)
            nc.vector.tensor_copy(gpT[:].rearrange("p t n -> p (t n)"), bank[2][:]).then_inc(g_pT[layer], 1)
            dve.wait_ge(g_o_ps[layer], r + 1)
            nc.vector.tensor_scalar(dst, o_ps, grec[:, 0:1], None, ALU.mult)

        def general_tensor(pe):
            with pe.Fori(0, B) as b:
                needed, k = turn(pe, b)
                f = k + 1
                with pe.If(needed > 0):
                    pe.wait_ge(g_in, f * 48)
                    for t in range(NT):
                        last = nc.tensor.transpose(bank[0][:, t * P:(t + 1) * P], gx[:, t, :], ident[:])
                    last.then_inc(g_xT_ps, 1)
                    pe.wait_ge(g_xT, f)
                    for g in range(G):
                        mm(bank[1 + g][:], wqTg[:, g, :], gxT[:])
                        mm(bank[1 + G + g][:], wkTg[:, g, :], gxT[:])
                    for t in range(NT):
                        last = mm(bank[1 + 2 * G][:, t * P:(t + 1) * P], gxT[:, t * P:(t + 1) * P], wvT[:])
                    last.then_inc(g_proj_ps, 1)
                    with pe.Fori(0, NT) as it:
                        t = k * NT + it
                        pe.wait_ge(g_proj, f)
                        pe.wait_ge(g_tile, t + 1)
                        for h in range(H):
                            r = t * H + h
                            c = 32 * (h % HG)
                            mm(bank[0][:], gqt[c:c + 32, h // HG, :], gk[c:c + 32, h // HG, :]).then_inc(g_score[0], 1)
                            pe.wait_ge(g_exp[0], r + 1)
                            for j in range(NT):
                                last = nc.tensor.transpose(bank[2][:, j * P:(j + 1) * P], gp[:, j * P:(j + 1) * P], ident[:])
                            last.then_inc(g_pT_ps[0], 1)
                            pe.wait_ge(g_pT[0], r + 1)
                            for j in range(NT):
                                last = mm(bank[3][:, h * HD:(h + 1) * HD], gpT[:, j, :], gv[:, j, h * HD:(h + 1) * HD],
                                          j == 0, j == NT - 1)
                            last.then_inc(g_o_ps[0], 1)
                        pe.wait_ge(g_o[0], t + 1)
                        nc.tensor.transpose(bank[5][:, 0:P], go[:], ident[:]).then_inc(g_oT_ps[0], 1)
                        pe.wait_ge(g_oT[0], t + 1)
                        mm(bank[4][:, 0:D], goT[:], woT[:]).then_inc(g_y_ps[0], 1)
                    pe.wait_ge(g_x1, f)
                    for t in range(NT):
                        last = nc.tensor.transpose(bank[0][:, t * P:(t + 1) * P], gx1[:, t, :], ident[:])
                    last.then_inc(g_x1T_ps, 1)
                    pe.wait_ge(g_x1T, f)
                    for jt in range(NT):
                        if jt:
                            pe.wait_ge(g_fp, k * NT + jt)
                        for half in range(2):
                            cols = slice(half * 512, half * 512 + 512)
                            mm(bank[1 + half][:], gxT[:, jt * P:(jt + 1) * P], fcw[:, cols], True, False)
                            last = mm(bank[1 + half][:], ones[0:1, :], fcb[0:1, cols], False, True)
                        last.then_inc(g_fp_ps, 1)
                    for h in range(H):
                        pe.wait_ge(g_diag, k * H + h + 1)
                        if h:
                            pe.wait_ge(g_krow, k * H + h)
                        mm(bank[3][:], ones[:], gdiag[:].rearrange("p t n -> p (t n)")).then_inc(g_krow_ps, 1)
                    with pe.Fori(0, NT) as it:
                        t = k * NT + it
                        for h in range(H):
                            r = t * H + h
                            pe.wait_ge(g_exp[1], r + 1)
                            for j in range(NT):
                                last = nc.tensor.transpose(bank[2][:, j * P:(j + 1) * P], gp[:, j * P:(j + 1) * P], ident[:])
                            last.then_inc(g_pT_ps[1], 1)
                            pe.wait_ge(g_pT[1], r + 1)
                            for j in range(NT):
                                last = mm(bank[3][:, 0:D], gpT[:, j, :], gfp[:, j, h * D:(h + 1) * D], j == 0, j == NT - 1)
                            last.then_inc(g_o_ps[1], 1)
                            pe.wait_ge(g_o[1], r + 1)
                            nc.tensor.transpose(bank[5][:, 0:P], go[:], ident[:]).then_inc(g_oT_ps[1], 1)
                            pe.wait_ge(g_oT[1], r + 1)
                            last = mm(bank[4][:, 0:D], goT[:], fpw[:, h, :], h == 0, h == H - 1)
                        last.then_inc(g_y_ps[1], 1)
                    pe.wait_ge(g_out, f * 16)



        class Graph:

            def __init__(self, base, off=0, eng=None, products=None):
                self.base, self.off, self.eng = base, off, eng
                self.static = isinstance(base, int)
                self.products = {} if products is None else products

            def up(self, k):
                return Graph(self.base, self.off + k, self.eng, self.products)

            def at(self, per, i, unit=1):
                if self.static:
                    return ((self.base + self.off) * per + i + 1) * unit
                if per * unit not in self.products:
                    self.products[per * unit] = self.eng.snap(self.base * (per * unit))
                return self.products[per * unit] + (self.off * per + i + 1) * unit

            @property
            def index(self):
                return bass.ds(self.base + self.off, 1)

        def bodies(eng, body, fold=None):
            def peeled(m):
                body(Graph(m), m % 2, *(0 <= m + rel < B for rel in (1, 0, -1, -2)))
            peeled(-1)
            if fold:
                fold(eng)
            peeled(0)
            peeled(1)
            with eng.Fori(2, B - 3, 2) as n:
                even = Graph(n, 0, eng)
                body(even, 0, True, True, True, True)
                body(even.up(1), 1, True, True, True, True)
            for m in range(B - 2, B + 2):
                peeled(m)

        USES = (
            ("xT", 1, p_act, 0, 8, 1), ("fold", 2, t_th, 0, 1, -2), ("q", 0, p_dve, 0, 6, 1), ("k", 1, p_dve, 1, 6, 1),
            ("t2g1", 0, normed, 1, 2, -1), ("v", 2, p_act, 3, 8, 1), ("a0", 1, p_act, 4, 8, 1), ("onT", 0, t_act, 1, 3, -1),
            ("a1", 2, p_act, 5, 8, 1), ("oh0", 1, m_act, 0, 3, 0), ("wo", 0, t_y, 0, 1, -1), ("a2", 2, p_act, 6, 8, 1),
            ("a3", 1, p_act, 7, 8, 1), ("oh1", 2, m_act, 2, 3, 0), ("t2g0", 1, normed, 0, 2, 0), ("gather", 0, t_act, 2, 3, -1))
        NAMES = [u[0] for u in USES]

        def bank_free(pe, name, n):
            i = NAMES.index(name)
            for turn_back, before in ((0, USES[:i]), (1, USES)):
                for _, used, s, ev, per, rel in reversed(before):
                    m = n.up(rel - turn_back)
                    if used == USES[i][1] and (not m.static or 0 <= m.base + m.off < B):
                        pe.wait_ge(s, m.at(per, ev))
                        return

        def rows(src, m):
            src = src[m.index] if not m.static else src[m.base + m.off:m.base + m.off + 1]
            return src.rearrange("o (t p) d -> p (o t) d", p=P)

        def mbank(name):
            return M_BANK[USES[NAMES.index(name)][1]]

        def mm(o, l, r, start=True, stop=True):
            return nc.tensor.matmul(o, l, r, start=start, stop=stop)

        def transpose_tensor(pe):
            pe.wait_ge(s_w2, 16 * OTHER_LOADS)
            for h in range(H):
                nc.tensor.transpose(bank[2 + h // 4][:, (h % 4) * P:(h % 4 + 1) * P], fcw[:, h * D:(h + 1) * D], ident[:])
            nc.tensor.transpose(bank[4][:, 0:H], fcb8[:], ident[0:H, 0:H]).then_inc(s_fcT_ps, 1)

        def fold_tensor(pe):
            pe.wait_ge(s_fcT, 1)
            for h in range(H):
                mm(bank[4][:, 2 * h:2 * h + 2], fcT[:, h, :], qkcol[:])
            for h in range(H):
                mm(bank[2][:, 0:D], fcT[:, h, :], fpw[:, h, :], h == 0, h == H - 1)
            for h in range(H):
                last = mm(bank[3][:, 0:D], fcB[:, h, :], fpw[:, h, :], h == 0, h == H - 1)
            last.then_inc(s_fold_ps, 1)
            pe.wait_ge(s_fold_in, 1)
            mm(bank[4][:, 0:4 * H], ones[:], nsq[:]).then_inc(s_norm_ps, 1)
            pe.wait_ge(s_norm, 1)

        def transpose_vector(dve):
            dve.wait_ge(s_fcT_ps, 1)
            nc.vector.tensor_copy(fcT[:, 0:4, :], bank[2][:].rearrange("p (h d) -> p h d", h=4))
            nc.vector.tensor_copy(fcT[:, 4:8, :], bank[3][:].rearrange("p (h d) -> p h d", h=4))
            nc.vector.tensor_copy(fcbT[:], bank[4][:, 0:H])
            dve.drain()
            for h in range(H):
                last = nc.vector.tensor_scalar(fcB[:, h, :], ones[:], fcbT[:, h:h + 1], None, ALU.mult)
            last.then_inc(s_fcT, 1)
            for a in range(2):
                nc.vector.tensor_scalar(nsq[:, 2 * H + a * H:2 * H + (a + 1) * H], fcbT[:], qkcol[:, a:a + 1], None, ALU.mult)
            nc.vector.memset(wqTg[:], 0.0)
            nc.vector.memset(wkTg[:], 0.0)
            dve.drain()
            for pad, w in ((wqTg, wqT), (wkTg, wkT)):
                nc.vector.tensor_copy(pad[:].rearrange("p g (c d) -> p (g c) d", d=32)[:, :, 0:HD],
                                      w[:].rearrange("p (h d) -> p h d", h=H))

        def fold_vector(dve):
            dve.wait_ge(s_fold_ps, 1)
            nc.vector.tensor_copy(fcqk[:].rearrange("p (a h) -> p a h", a=2),
                                  bank[4][:, 0:2 * H].rearrange("p (h a) -> p a h", a=2))
            nc.vector.tensor_copy(wf[:], bank[2][:, 0:D])
            nc.vector.tensor_tensor(bf[:], bank[3][:, 0:D], fpb[:], ALU.add)
            dve.drain()
            nc.vector.tensor_tensor(nsq[:, 0:2 * H], fcqk[:], fcqk[:], ALU.mult).then_inc(s_fold_in, 1)
            dve.wait_ge(s_norm_ps, 1)
            nc.vector.tensor_copy(nsq[:], bank[4][:, 0:4 * H]).then_inc(s_norm, 1)

        def fold_gpsimd(pool):
            pool.wait_ge(s_norm, 1)
            nc.gpsimd.tensor_tensor(nrm[:, 0:2 * H], nsq[:, 0:2 * H], phalf[:], ALU.pow).then_inc(s_root, 1)

        def least_gap(dve):
            for a in range(2):
                nc.vector.tensor_scalar(nsq[:, 2 * H + a * H:2 * H + (a + 1) * H], nsq[:, 2 * H + a * H:2 * H + (a + 1) * H],
                                        qkb[:, a:a + 1], None, ALU.add)
            dve.drain()
            nc.vector.tensor_scalar(nab[:], nsq[:, 2 * H:4 * H], -1.0, None, ALU.mult)
            dve.drain()
            nc.vector.tensor_tensor(nab[:], nab[:], nsq[:, 2 * H:4 * H], ALU.max)
            dve.drain()
            dve.wait_ge(s_root, 1)
            nc.vector.scalar_tensor_tensor(nab[:], nrm[:], 1.02 * float(D) ** 0.5, nab[:], ALU.mult, ALU.add)
            dve.drain()
            nc.vector.tensor_reduce(gst[:, 0:2], nab[:].rearrange("p (a h) -> p a h", a=2), AX_X, ALU.max)
            dve.drain()
            nc.vector.tensor_tensor(gst[:, 2:3], gst[:, 0:1], gst[:, 1:2], ALU.add)
            dve.drain()
            nc.vector.tensor_scalar(gapmin[:], gst[:, 2:3], 2.04, 112.0, ALU.mult, ALU.add)

        def fast_tensor(pe, n, p, nxt, main, bef, bef2):
            def scores(m, s, par):
                g, jp, c = s // RING, (s // HG) % 2, s % HG
                h = g * HG + c
                if s == 0:
                    pe.wait_ge(stack_in, m.at(12, 11, 16))
                if not (m.static and m.base + m.off == 0 and s < 2):
                    pe.wait_ge(biased, m.at(STEPS, s - 2))
                for e in range(2):
                    jt = 2 * jp + e
                    last = mm(S_PS[s % 2][:, e, :], QK[par][0:KR, 1, h, jt * P:(jt + 1) * P], QK[par][0:KR, 0, h, :])
                last.then_inc(qk_ready, 1)

            def values(m, block, e, par):
                g, jt = block // 2, (block % 2) * 2 + e
                pe.wait_ge(exped, m.at(STEPS, HG * block + HG - 1))
                if jt == 0:
                    if g == 1:
                        pe.wait_ge(m_act, m.at(3, 1))
                    elif not (m.static and m.base + m.off == 0):
                        pe.wait_ge(t_act, m.up(-1).at(3, 0))
                for c in range(HG):
                    last = nc.tensor.matmul(O_BANK[32 * c:32 * c + 32, :], V[par][:, jt, g * HG + c, :],
                                            TE[(HG * block + c) % RING][:, e, :], start=jt == 0, stop=jt == NT - 1,
                                            tile_position=(0, 32 * c))
                last.then_inc(pv_done, 1)

            def shared(name, when=True):
                if when:
                    bank_free(pe, name, n)
                return when

            nx, pv, pv2 = n.up(1), n.up(-1), n.up(-2)

            def adjT(j):
                if shared(f"a{j}", nxt):
                    pe.wait_ge(a_in, nx.at(1, 0, 16))
                    for t in range(NT):
                        last = nc.tensor.transpose(mbank(f"a{j}")[:, t * P:(t + 1) * P],
                                                   A[1 - p][:, t, j * P:(j + 1) * P], ident[:])
                    last.then_inc(p_full, 1)

            def onehotT(k):
                if shared(f"oh{k}", main):
                    pe.wait_ge(onehot, n.at(4, 3))
                    o = mbank(f"oh{k}")[:].bitcast(bf16)
                    for j in range(2):
                        for t in range(NT):
                            last = nc.tensor.transpose(o[:, j * N + t * P:j * N + (t + 1) * P],
                                                       OH[:, t, (2 * k + j) * P:(2 * k + j + 1) * P], identb[:])
                    last.then_inc(m_full, 1)

            for s in range(STEPS):
                if main and s < STEPS - 1:
                    scores(n, s + 1, p)
                if s == STEPS - 1 and n.static and n.base + n.off == -1:
                    fold_tensor(pe)
                if s == STEPS - 1 and nxt:
                    scores(nx, 0, 1 - p)
                if s == 2 and shared("q", nxt):
                    pe.wait_ge(p_act, nx.at(8, 0))
                    mm(mbank("q")[:], wqT[:], XT[:]).then_inc(p_full, 1)
                if bef and s in (1, 2):
                    values(pv, 3, s - 1, 1 - p)
                if main and s >= 5 and s % HG in (1, 2):
                    values(n, (s - 5) // HG, s % HG - 1, p)
                if s == 0 and shared("xT", nxt):
                    pe.wait_ge(x_in, nx.at(1, 0, 16))
                    for t in range(NT):
                        last = nc.tensor.transpose(mbank("xT")[:, t * P:(t + 1) * P], X[:, t, :], ident[:])
                    last.then_inc(p_full, 1)
                if s == 0 and shared("fold", bef2):
                    pe.wait_ge(t_xb, pv2.at(1, 0))
                    mm(mbank("fold")[:], ident[:], XB[:].rearrange("p t d -> p (t d)"), True, False)
                if s == 1 and bef2:
                    pe.wait_ge(t_act, pv2.at(3, 2))
                    for t in range(NT):
                        last = mm(mbank("fold")[:, t * P:(t + 1) * P], GT[:, t * P:(t + 1) * P], wf[:], False, t == NT - 1)
                    last.then_inc(t_full, 1)
                if s == 3 and shared("k", nxt):
                    mm(mbank("k")[:], wkT[:], XT[:]).then_inc(p_full, 1)
                if s == 4 and shared("t2g1", bef):
                    pe.wait_ge(t_act, pv.at(3, 0))
                    for t in range(NT):
                        last = nc.tensor.transpose(mbank("t2g1")[:, t * P:(t + 1) * P], OS[:, 1, t * P:(t + 1) * P], ident[:])
                    last.then_inc(t_full, 1)
                if s == 4 and shared("v", nxt):
                    for t in range(NT):
                        last = mm(mbank("v")[:, t * P:(t + 1) * P], XT[:, t * P:(t + 1) * P], wvT[:])
                    last.then_inc(p_full, 1)
                if s == 4 and n.static and n.base + n.off == -1:
                    transpose_tensor(pe)
                if s == 5:
                    adjT(0)
                if s == 6 and shared("onT", bef):
                    pe.wait_ge(normed, pv.at(2, 1))
                    for t in range(NT):
                        last = nc.tensor.transpose(mbank("onT")[:, t * P:(t + 1) * P],
                                                   ON[:, t, :, :].rearrange("p h d -> p (h d)"), ident[:])
                    last.then_inc(t_full, 1)
                if s == 6:
                    adjT(1)
                if s == 7:
                    onehotT(0)
                if s == 7 and shared("wo", bef):
                    pe.wait_ge(xr_in, pv.at(1, 0, 16))
                    mm(mbank("wo")[:], ident[:], XR[:].rearrange("p t d -> p (t d)"), True, False)
                    pe.wait_ge(t_act, pv.at(3, 1))
                    for t in range(NT):
                        last = mm(mbank("wo")[:, t * P:(t + 1) * P], ONT[:, t * P:(t + 1) * P], woT[:], False, t == NT - 1)
                    last.then_inc(t_full, 1)
                if s == 8:
                    adjT(2)
                if s == 9:
                    adjT(3)
                if s == 11:
                    onehotT(1)
                if s == 12 and shared("t2g0", main):
                    pe.wait_ge(m_act, n.at(3, 1))
                    for t in range(NT):
                        last = nc.tensor.transpose(mbank("t2g0")[:, t * P:(t + 1) * P], OS[:, 0, t * P:(t + 1) * P],
                                                   ident[:])
                    last.then_inc(m_full, 1)
                if s >= 13 and bef:
                    k = s - 13
                    if k == 0:
                        shared("gather")
                        pe.wait_ge(m_act, pv.at(3, 2))
                    pe.wait_ge(t_cs, pv.at(3, k))
                    for j in range(NT):
                        last = mm(mbank("gather")[:], CS[:, k, j, :], PT[1 - p][:, j, :], k == 0 and j == 0,
                                  k == 2 and j == NT - 1)
                    if k == 2:
                        last.then_inc(t_full, 1)
                if bef2 and not bef and s == 2:
                    pe.wait_ge(s_bad, 1)
                    mm(bank[0][0:B, 0:1], checks[:], ones[:, 0:1]).then_inc(s_cnt_ps, 1)
                    pe.wait_ge(s_cnt, 1)
                    mm(bank[1][0:1, 0:2 * B + 1], fcol[:], tri[:]).then_inc(s_ord_ps, 1)

        def fast_scalar(act, n, p, nxt, main, bef, bef2):
            nx, pv, pv2 = n.up(1), n.up(-1), n.up(-2)

            def take(per, sem_, ev, m, out_, in_, done):
                act.wait_ge(sem_, m.at(per, ev))
                nc.scalar.copy(out_, in_).then_inc(done, 1)

            def adjT(j):
                if nxt:
                    take(8, p_full, 4 + j, nx, AT[1 - p][:, 0, j, :], mbank(f"a{j}")[:], p_act)

            def others(m, t, q):
                act.wait_ge(maxed, m.at(4, t))
                if t == 0 and not (m.static and m.base + m.off == 0):
                    act.wait_ge(m_full, m.up(-1).at(3, 1))
                nc.scalar.activation(OH[:, t, :], A[q][:, t, :], ACT.Sign, bias=MX[q][:, t, 0:1], scale=-1.0).then_inc(onehot, 1)

            def onehotT(k):
                if main:
                    act.wait_ge(m_full, n.at(3, k))
                    nc.scalar.activation(PT[p][:, 2 * k:2 * k + 2, :].rearrange("p t n -> p (t n)"),
                                         mbank(f"oh{k}")[:].bitcast(bf16), ACT.Identity, bias=ones[:, 0:1],
                                         scale=-1.0).then_inc(m_act, 1)

            for s in range(STEPS):
                if main:
                    act.wait_ge(biased, n.at(STEPS, s))
                    nc.scalar.activation(TE[s % RING][:], TE[s % RING][:], ACT.Exp).then_inc(exped, 1)
                if s == 0 and nxt:
                    take(8, p_full, 0, nx, XT[:], mbank("xT")[:], p_act)
                if s == 1 and bef2:
                    act.wait_ge(t_full, pv2.at(5, 4))
                    nc.scalar.activation(TH[:].rearrange("p t d -> p (t d)"), mbank("fold")[:], ACT.Tanh,
                                         scale=0.5).then_inc(t_th, 1)
                if s == 2 and nxt:
                    if not (n.static and n.base + n.off == -1):
                        act.wait_ge(spl_out, n.at(1, 0, 16))
                    take(8, p_full, 1, nx, SPL[:, 0, 0, :], mbank("q")[:], p_act)
                if s == 2 and bef:
                    take(8, pv_done, 7, pv, OS[:, 1, :], O_BANK[:], t_act)
                if s == 3 and nxt:
                    take(8, p_full, 2, nx, SPL[:, 1, 0, :], mbank("k")[:], p_act)
                if s == 4 and nxt:
                    act.wait_ge(p_full, nx.at(8, 3))
                    act.wait_ge(s_vones, 1)
                    nc.scalar.copy(V[1 - p][:, :, :, 0:HD].rearrange("p t h d -> p (t h) d"),
                                   mbank("v")[:].rearrange("p (h d) -> p h d", d=HD)).then_inc(p_act, 1)
                if s == 4 and main:
                    others(n, 2, p)
                if s == 5:
                    adjT(0)
                    if main:
                        others(n, 3, p)
                if s == 5 and bef:
                    take(5, t_full, 1, pv, ONT[:], mbank("onT")[:], t_act)
                if s == 6:
                    adjT(1)
                if s == 7 and bef:
                    take(5, t_full, 2, pv, Y[:].rearrange("p t d -> p (t d)"), mbank("wo")[:], t_y)
                if s == 7:
                    onehotT(0)
                if s == 8:
                    adjT(2)
                if s == 9:
                    adjT(3)
                if s == 10 and main:
                    take(8, pv_done, 3, n, OS[:, 0, :], O_BANK[:], m_act)
                if s == 11:
                    onehotT(1)
                if s in (12, 14) and nxt:
                    others(nx, (12, 14).index(s), 1 - p)
                if s == 15 and bef:
                    take(5, t_full, 3, pv, GT[:], mbank("gather")[:], t_act)

        def which_need_general(dve):
            m2, b2, l2, w2 = CK
            least_gap(dve)
            dve.drain()
            nc.vector.tensor_scalar(m2, tops[:], -1.0, 1.0, ALU.mult, ALU.add)
            dve.drain()
            nc.vector.tensor_scalar(b2, m2, NEG, None, ALU.mult)
            dve.drain()
            nc.vector.tensor_scalar(w2, b2, 0.0, None, ALU.max)
            nc.vector.tensor_scalar(m2, b2, 0.0, None, ALU.min)
            dve.drain()
            nc.vector.tensor_scalar(l2, m2, 0.01, None, ALU.mult)
            nc.vector.tensor_tensor(b2, w2, m2, ALU.subtract)
            dve.drain()
            nc.vector.tensor_tensor(l2, l2, w2, ALU.add)
            nc.vector.tensor_tensor(b2[:, :, :, 0], b2[:, :, :, 0], b2[:, :, :, 1], ALU.add)
            dve.drain()
            nc.vector.tensor_tensor(l2[:, :, :, 0], l2[:, :, :, 0], l2[:, :, :, 1], ALU.subtract)
            nc.vector.tensor_scalar(b2[:, :, :, 0], b2[:, :, :, 0], 2.0 ** -21, None, ALU.mult)
            dve.drain()
            nc.vector.tensor_scalar(b2[:, :, :, 0], b2[:, :, :, 0], gapmin[:, 0:1], None, ALU.add)
            dve.drain()
            nc.vector.tensor_tensor(w2[:, :, :, 0], l2[:, :, :, 0], b2[:, :, :, 0], ALU.is_ge)
            nc.vector.tensor_scalar(CR2, denoms[:], 1e20, None, ALU.is_le)
            dve.drain()
            nc.vector.scalar_tensor_tensor(CR2, denoms[:], 1e-30, CR2, ALU.is_ge, ALU.mult)
            nc.vector.tensor_reduce(checks[:], w2[:, :, :, 0], AX_X, ALU.min)
            dve.drain()
            nc.vector.tensor_reduce(fine[:], CR2, AX_X, ALU.min)
            nc.vector.tensor_scalar(checks[:], checks[:], weok[:, 0:1], None, ALU.mult)
            dve.drain()
            nc.vector.tensor_tensor(checks[:], checks[:], fine[:], ALU.mult)
            dve.drain()
            nc.vector.tensor_scalar(checks[:], checks[:], -1.0, 1.0, ALU.mult, ALU.add).then_inc(s_bad, 1)

        def flag_graphs(dve):
            dve.wait_ge(s_cnt_ps, 1)
            nc.vector.tensor_scalar(fcol[:], bank[0][0:B, 0:1], 0.5, None, ALU.is_ge).then_inc(s_cnt, 1)
            dve.wait_ge(s_ord_ps, 1)
            nc.vector.tensor_copy(flags[:], bank[1][0:1, 0:2 * B + 1]).then_inc(s_flags, 1)

        def where_needed(eng, general):
            eng.wait_ge(s_flags, 1)
            how_many = eng.value_load(flags[0:1, 2 * B:2 * B + 1], min_val=0, max_val=B)
            with eng.If(how_many > 0):
                general(eng)

        def fast_vector(dve, n, p, nxt, main, bef, bef2):
            nx, pv, pv2 = n.up(1), n.up(-1), n.up(-2)

            def bias(s):
                g, jp, c = s // RING, (s // HG) % 2, s % HG
                h = g * HG + c
                if s == 11 and nxt:
                    dve.wait_ge(a_in, nx.at(1, 0, 16))
                if s % HG == 0:
                    if g == 0:
                        dve.wait_ge(p_pool, n.at(6, 2 + 2 * jp + 1))
                    if not (n.static and n.base + n.off == 0 and s < RING):
                        dve.wait_ge(pv_done, n.at(8, 2 * ((s - RING) // HG) + 1))
                dve.wait_ge(qk_ready, n.at(STEPS, s))
                flat = AT[p][:].rearrange("p a t n -> p (a t n)")
                nc.vector.scalar_tensor_tensor(TE[s % RING][:].rearrange("p e n -> p (e n)"),
                                               flat[:, bass.ds(signs[h] + 2 * jp * N, 2 * N)], we[:, h:h + 1],
                                               S_PS[s % 2][:].rearrange("p e n -> p (e n)"), ALU.mult, ALU.add).then_inc(biased, 1)

            def largest(m, t, q):
                if t == 0 and m.static:
                    dve.wait_ge(a_in, m.at(1, 0, 16))
                nc.vector.max(MX[q][:, t, :], A[q][:, t, :]).then_inc(maxed, 1)

            def residual(a):
                if nxt:
                    dve.wait_ge(p_act, nx.at(8, 1 + a))
                    nc.vector.tensor_tensor(RES[:, a, :], mbank("qk"[a])[:], SPL[:, a, 0, :], ALU.subtract).then_inc(p_dve, 1)

            def outputs(name):
                return mbank(name)[:].rearrange("p (t h c) -> p t h c", t=NT, h=HG)

            def reciprocals(g, m, rd, name, full, per, ev):
                dve.wait_ge(full, m.at(per, ev))
                nc.vector.reciprocal(rd[:, g, :, :], outputs(name)[:, :, :, HD]).then_inc(recip, 1)

            def normalise(g, m, rd, name):
                dve.wait_ge(recip, m.at(2, g))
                nc.vector.tensor_tensor(ON[:, :, g * HG:(g + 1) * HG, :], outputs(name)[:, :, :, 0:HD],
                                        rd[:, g, :, :].rearrange("p t (h o) -> p t h o", o=1).to_broadcast([P, NT, HG, HD]),
                                        ALU.mult).then_inc(normed, 1)

            def statistics(layer, src, m, made):
                dve.wait_ge(made, m.at(1, 0))
                for t in range(NT):
                    nc.vector.bn_stats(ST[:, layer, t, :], src[:, t, :])

            def means(layer):
                dve.drain()
                for t in range(NT):
                    last = nc.vector.bn_aggr(MV[:, layer, t, :], ST[:, layer, t, :])
                last.then_inc(t_mv, 1)

            def zeros(j):
                if nxt:
                    dve.wait_ge(p_act, nx.at(8, 4 + j))
                    nc.vector.tensor_scalar(MT[:, j, :], AT[1 - p][:, 0, j, :], 0.0, -BIG, ALU.is_equal,
                                            ALU.mult).then_inc(p_dve, 1)

            def last_scale(layer, dst, src, done):
                dve.wait_ge(t_rs, layer + 1)
                for t in range(NT):
                    last = nc.vector.tensor_scalar(dst[:, t, :], src[:, t, :], MV[:, layer, t, 0:1], RS[:, layer, t:t + 1],
                                                   ALU.subtract, ALU.mult)
                last.then_inc(done, 1)

            def last_split():
                flat = lambda m: m[:].rearrange("p t d -> p (t d)")
                dve.drain()
                nc.vector.tensor_copy(flat(CS[:, 0]), flat(X1)).then_inc(t_cs, 1)
                dve.drain()
                nc.vector.tensor_tensor(flat(CR), flat(X1), flat(CS[:, 0]), ALU.subtract)
                dve.drain()
                nc.vector.tensor_copy(flat(CS[:, 1]), flat(CR)).then_inc(t_cs, 1)
                dve.drain()
                nc.vector.tensor_tensor(flat(CS[:, 2]), flat(CR), flat(CS[:, 1]), ALU.subtract).then_inc(t_cs, 1)
                nc.vector.tensor_tensor(XB[:], X1[:], bf[:].rearrange("p (o d) -> p o d", o=1).to_broadcast([P, NT, D]),
                                        ALU.add).then_inc(t_xb, 1)
                nc.vector.tensor_scalar(flat(XH), flat(X1), 0.5, None, ALU.add).then_inc(t_xh, 1)

            for s in range(STEPS):
                if main:
                    bias(s)
                if s == 0 and main:
                    largest(n, 2, p)
                if s == 1 and main:
                    largest(n, 3, p)
                if s == 3:
                    residual(0)
                if s == 4:
                    if bef2:
                        dve.wait_ge(t_th, pv2.at(1, 0))
                        dve.wait_ge(t_xh, pv2.at(1, 0))
                        nc.vector.scalar_tensor_tensor(U[:].rearrange("p t d -> p (t d)"),
                                                       TH[:].rearrange("p t d -> p (t d)"), 0.5,
                                                       XH[:].rearrange("p t d -> p (t d)"), ALU.mult, ALU.add).then_inc(t_u, 1)
                    residual(1)
                if s == 4 and n.static and n.base + n.off == -1:
                    transpose_vector(dve)
                if s == 5:
                    if bef:
                        reciprocals(1, pv, RD[1 - p], "t2g1", t_full, 5, 0)
                    if bef2:
                        statistics(1, U, pv2, t_u)
                    if bef:
                        normalise(1, pv, RD[1 - p], "t2g1")
                if s == 6:
                    zeros(0)
                    if bef2:
                        means(1)
                if s == 7:
                    zeros(1)
                if s == 8:
                    if main:
                        nc.vector.tensor_copy(tops[:, n.index, :, :].rearrange("p o t k -> p (o t) k"), MX[p][:, :, 0:2])
                    if bef:
                        nc.vector.tensor_copy(denoms[:, pv.index, :].rearrange("p o r -> p (o r)"),
                                              RD[1 - p][:].rearrange("p g t h -> p (g t h)"))
                    if bef and not main:
                        which_need_general(dve)
                    if bef:
                        statistics(0, Y, pv, t_y)
                if s == 9:
                    if bef:
                        means(0)
                    zeros(2)
                if s == 13:
                    zeros(3)
                if s in (11, 13) and nxt:
                    largest(nx, (11, 13).index(s), 1 - p)
                if s == 13 and main:
                    reciprocals(0, n, RD[p], "t2g0", m_full, 3, 2)
                if s == 14 and main:
                    normalise(0, n, RD[p], "t2g0")
                if s == 9 and bef and not main:
                    last_scale(0, X1, Y, t_x1)
                    last_split()
                if s == 7 and bef2 and not bef:
                    flag_graphs(dve)
                    last_scale(1, OUT, U, t_out)

        def fast_gpsimd(pool, n, p, nxt, main, bef, bef2):
            nx, pv, pv2 = n.up(1), n.up(-1), n.up(-2)
            G_ = nc.gpsimd

            def alone(m):
                if not m.static:
                    G_.tensor_tensor(CD[:], mhalf[:, 0:1], mhalf[:, 0:1], ALU.mult)

            flat = lambda m: m[:].rearrange("p t d -> p (t d)")
            if nxt:
                for a in range(2):
                    pool.wait_ge(p_dve, nx.at(6, a))
                    alone(n)
                    G_.tensor_scalar(SPL[:, a, 1, :], RES[:, a, :], 1.0, 0.0, ALU.mult, ALU.add)
                    pool.drain()
                    G_.tensor_tensor(SPL[:, a, 2, :], RES[:, a, :], SPL[:, a, 1, :], ALU.subtract).then_inc(p_pool, 1)

            def scale(layer, dst, src, done):
                pool.wait_ge(t_mv, (pv, pv2)[layer].at(2, layer))
                alone(n)
                G_.tensor_scalar(VAR[:, layer, :], MV[:, layer, :, 1], 1.0, EPS, ALU.mult, ALU.add)
                G_.tensor_scalar(NM[:, layer, :], MV[:, layer, :, 0], -1.0, 0.0, ALU.mult, ALU.add)
                pool.drain()
                G_.tensor_tensor(RS[:, layer, :], VAR[:, layer, :], mhalf[:, 0:NT], ALU.pow)
                pool.drain()
                for t in range(NT):
                    last = G_.tensor_scalar(dst[:, t, :], src[:, t, :], NM[:, layer, t:t + 1], RS[:, layer, t:t + 1],
                                            ALU.add, ALU.mult)
                last.then_inc(done, 1)

            def last_root(layer, m):
                pool.wait_ge(t_mv, m.at(2, layer))
                G_.tensor_scalar(VAR[:, layer, :], MV[:, layer, :, 1], 1.0, EPS, ALU.mult, ALU.add)
                pool.drain()
                G_.tensor_tensor(RS[:, layer, :], VAR[:, layer, :], mhalf[:, 0:NT], ALU.pow).then_inc(t_rs, 1)

            def masked(j):
                if nxt:
                    pool.wait_ge(p_dve, nx.at(6, 2 + j))
                    G_.tensor_tensor(AT[1 - p][:, 1, j, :], AT[1 - p][:, 0, j, :], MT[:, j, :], ALU.subtract)
                    pool.drain()
                    G_.tensor_tensor(AT[1 - p][:, 0, j, :], AT[1 - p][:, 0, j, :], MT[:, j, :], ALU.add).then_inc(p_pool, 1)

            masked(0)
            if bef2 and not bef:
                last_root(1, pv2)
            elif bef2:
                scale(1, OUT, U, t_out)
            if bef and not main:
                last_root(0, pv)
            elif bef:
                scale(0, X1, Y, t_x1)
                pool.drain()
                G_.tensor_scalar(flat(CS[:, 0]), flat(X1), 1.0, 0.0, ALU.mult, ALU.add).then_inc(t_cs, 1)
                pool.drain()
                G_.tensor_tensor(flat(CR), flat(X1), flat(CS[:, 0]), ALU.subtract)
                pool.drain()
                G_.tensor_scalar(flat(CS[:, 1]), flat(CR), 1.0, 0.0, ALU.mult, ALU.add).then_inc(t_cs, 1)
                pool.drain()
                G_.tensor_tensor(flat(CS[:, 2]), flat(CR), flat(CS[:, 1]), ALU.subtract).then_inc(t_cs, 1)
            masked(1)
            if bef and main:
                G_.tensor_tensor(XB[:], X1[:], bf[:].rearrange("p (o d) -> p o d", o=1).to_broadcast([P, NT, D]),
                                 ALU.add).then_inc(t_xb, 1)
            masked(2)
            masked(3)
            if bef and main:
                G_.tensor_scalar(flat(XH), flat(X1), 1.0, 0.5, ALU.mult, ALU.add).then_inc(t_xh, 1)
            if bef2:
                pool.wait_ge(out_st, pv2.at(1, 0, 16))

        def fast_sync(sp, n, p, nxt, main, bef, bef2):
            nx, pv, pv2 = n.up(1), n.up(-1), n.up(-2)
            first = n.static and n.base + n.off == -1
            second = n.static and n.base + n.off == 0
            at = lambda m, *a: m.at(*a) if m.static else sp.snap(m.at(*a))
            pv_first = pv.static and pv.base + pv.off == 0
            if nxt:
                x_free = at(n, 8, 0)
                parts_made, parts_out = at(nx, 6, 1), at(nx, 1, 0, 16)
                if not first and not second:
                    onehots, scored = at(n.up(-1), 4, 3), at(n, STEPS, 0)
            if bef and not pv_first:
                added = at(pv2, 1, 0)
            if bef2:
                result = at(pv2, 1, 0)
            if nxt:
                if not first:
                    sp.wait_ge(p_full, x_free)
                sp.dma_start(X[:], rows(x, nx)).then_inc(x_in, 16)
                if second:
                    sp.wait_ge(s_fold_ps, 1)
                if not first and not second:
                    sp.wait_ge(onehot, onehots)
                sp.dma_start(A[1 - p][:], rows(adj, nx)).then_inc(a_in, 16)
            if first:
                sp.dma_start(fcw[:], fc_w).then_inc(s_w2, 16)
                sp.dma_start(fcb8[:], fc_b.rearrange("(h n) -> h n", h=H)).then_inc(s_w2, 16)
                sp.dma_start(fpw[:], fp_w.rearrange("(h c) n -> c h n", h=H)).then_inc(s_w2, 16)
                sp.dma_start(fpb[:], fp_b.rearrange("(o n) -> o n", o=1).to_broadcast([P, D])).then_inc(s_w2, 16)
                sp.dma_start(qw[:], q_w.rearrange("n o -> o n").to_broadcast([P, D])).then_inc(s_w2, 16)
                sp.dma_start(kw[:], k_w.rearrange("n o -> o n").to_broadcast([P, D])).then_inc(s_w2, 16)
                sp.dma_start(qkcol[:, 0:1], q_w).then_inc(s_w2, 16)
                sp.dma_start(qkcol[:, 1:2], k_w).then_inc(s_w2, 16)
                sp.dma_start(qkb[:, 0:1], q_b.rearrange("(o n) -> o n", o=1).to_broadcast([P, 1])).then_inc(s_w2, 16)
                sp.dma_start(qkb[:, 1:2], k_b.rearrange("(o n) -> o n", o=1).to_broadcast([P, 1])).then_inc(s_w2, 16)
            if bef:
                if not pv_first:
                    sp.wait_ge(t_y, added)
                sp.dma_start(XR[:], rows(x, pv)).then_inc(xr_in, 16)
            if nxt:
                sp.wait_ge(p_pool, parts_made)
                sp.dma_start(scratch[1 - p], SPL[:]).then_inc(spl_out, 16)
                sp.wait_ge(spl_out, parts_out)
                if not first and not second:
                    sp.wait_ge(qk_ready, scored)
                for r, parts in enumerate(PARTS):
                    for a in range(2):
                        sp.dma_start(QK[1 - p][HD * r:HD * r + HD, a, :, :],
                                     scratch[1 - p, :, a, parts[a], :].rearrange("(h d) i -> d h i", h=H)).then_inc(stack_in, 16)
            if bef2:
                sp.wait_ge(t_out, result)
                sp.dma_start(rows(out, pv2), OUT[:]).then_inc(out_st, 16)

        block = ctx.enter_context(nc.Block())

        @block.sync
        def _(sp):
            for dst, src in ((wq_rows, W_q), (wk_rows, W_k), (wv_rows, W_v), (wo_rows, W_o)):
                sp.dma_start(dst, src).then_inc(s_w, 16)
            sp.dma_start(we[:], W_e.rearrange("h o -> o h").to_broadcast([P, H])).then_inc(s_w, 16)
            bodies(sp, lambda *a: fast_sync(sp, *a))
            last = Graph(B - 1)
            sp.wait_ge(out_st, last.at(1, 0, 16))
            where_needed(sp, general_sync)

        @block.gpsimd
        def _(pool):
            pool.memset(ident[:], 0.0).then_inc(s_c, 1)
            pool.memset(tri[:, 0:2 * B], 0.0).then_inc(s_c, 1)
            pool.wait_ge(s_c, 2)
            pool.affine_select(out=ident[:], in_=ident[:], compare_op=ALU.not_equal, fill=1.0, base=0,
                               pattern=[[-1, P]], channel_multiplier=1).then_inc(s_c, 1)
            pool.affine_select(out=tri[:, 0:B], in_=tri[:, 0:B], compare_op=ALU.not_equal, fill=1.0, base=0,
                               pattern=[[-1, B]], channel_multiplier=1).then_inc(s_c, 1)
            pool.affine_select(out=tri[:, B:2 * B], in_=tri[:, B:2 * B], compare_op=ALU.is_ge, fill=1.0, base=0,
                               pattern=[[-1, B]], channel_multiplier=1).then_inc(s_c, 1)
            pool.memset(tri[:, 2 * B:2 * B + 1], 1.0).then_inc(s_c, 1)
            pool.memset(ones[:], 1.0).then_inc(s_c, 1)
            pool.memset(mhalf[:], -0.5).then_inc(s_c, 1)
            pool.memset(phalf[:], 0.5).then_inc(s_c, 1)
            for i in range(2):
                last = pool.memset(V[i][:], 1.0)
            last.then_inc(s_vones, 1)
            bodies(pool, lambda *a: fast_gpsimd(pool, *a), fold_gpsimd)
            where_needed(pool, general_gpsimd)

        @block.scalar
        def _(act):
            act.wait_ge(s_c, 9)
            nc.scalar.activation(warm[:], mhalf[:, 0:1], ACT.Exp)
            bodies(act, lambda *a: fast_scalar(act, *a))
            where_needed(act, general_scalar)

        @block.vector
        def _(dve):
            dve.wait_ge(s_wT_ps, 1)
            nc.vector.tensor_scalar(wqT[:], bank[0][:, 0:P], float(HD) ** -0.5, None, ALU.mult)
            nc.vector.tensor_copy(wkT[:], bank[0][:, P:2 * P])
            nc.vector.tensor_copy(wvT[:], bank[0][:, 2 * P:3 * P])
            nc.vector.tensor_copy(woT[:], bank[0][:, 3 * P:4 * P]).then_inc(s_const, 1)
            nc.vector.tensor_scalar(sgn[0:1, 0:H], we[0:1, :], 0.0, float(NT * N), ALU.is_lt, ALU.mult)
            nc.vector.tensor_tensor(wesq[:], we[:], we[:], ALU.mult)
            nc.vector.tensor_copy(identb[:], ident[:])
            dve.drain()
            nc.vector.tensor_reduce(gst[:, 3:4], wesq[:], AX_X, ALU.min)
            dve.drain()
            nc.vector.tensor_scalar(weok[:], gst[:, 3:4], 1e-20, None, ALU.is_ge)
            dve.drain()
            for h in range(H):
                signs.append(dve.value_load(sgn[0:1, h:h + 1], min_val=0, max_val=NT * N))
            bodies(dve, lambda *a: fast_vector(dve, *a), fold_vector)
            where_needed(dve, general_vector)

        @block.tensor
        def _(pe):
            pe.wait_ge(s_c, 9)
            pe.wait_ge(s_w, 16 * WEIGHT_LOADS)
            for i, w in enumerate((wq_rows, wk_rows, wv_rows, wo_rows)):
                last = nc.tensor.transpose(bank[0][:, i * P:(i + 1) * P], w, ident[:])
            last.then_inc(s_wT_ps, 1)
            pe.wait_ge(s_const, 1)
            bodies(pe, lambda *a: fast_tensor(pe, *a))
            where_needed(pe, general_tensor)


_INS = ['x', 'adj', 'L0_gnn_W_q', 'L0_gnn_W_k', 'L0_gnn_W_v', 'L0_gnn_W_e', 'L0_gnn_W_o', 'L1_gnn_fc_w', 'L1_gnn_fc_b',
        'L1_gnn_q_w', 'L1_gnn_q_b', 'L1_gnn_k_w', 'L1_gnn_k_b', 'L1_gnn_fp_w', 'L1_gnn_fp_b']


def kernel(**inputs):
    import numpy as _np
    import concourse.bacc as _bacc
    from concourse import mybir as _mybir
    from concourse.bass_utils import run_bass_kernel_spmd as _run

    nc = _bacc.Bacc("TRN2", target_bir_lowering=False, num_devices=1)
    arrays, args = {}, []
    for name in _INS:
        a = _np.ascontiguousarray(inputs[name])
        arrays[f"in_{name}_dram"] = a
        args.append(nc.dram_tensor(f"in_{name}_dram", a.shape, _mybir.dt.from_np(a.dtype), kind="ExternalInput").ap())
    o = nc.dram_tensor("out_0_dram", inputs["x"].shape, _mybir.dt.float32, kind="ExternalOutput").ap()
    gnn_kernel(nc, *args, o)
    r = _run(nc, [arrays], core_ids=[0])
    return r.results[0]["out_0_dram"]
```
